# Optimizing a Trainium2 kernel written in Bass

```python
import numpy as np
import jax
import jax.numpy as jnp

def _softmax(x, axis=-1):
    return jax.nn.softmax(x, axis=axis)

def _gelu(x):
    return jax.nn.gelu(x, approximate=True)

def _silu(x):
    return jax.nn.silu(x)

def _sigmoid(x):
    return jax.nn.sigmoid(x)

def _layernorm(x, axis=-1, eps=1e-05):
    m = jnp.mean(x, axis=axis, keepdims=True)
    v = jnp.var(x, axis=axis, keepdims=True)
    return (x - m) / jnp.sqrt(v + eps)

def _scatter_add(tgt, idx, src, axis=0):
    return tgt.at[idx].add(src)

def _segment_sum(src, seg, n):
    return jax.ops.segment_sum(src, seg, n)
kernel_name = 'mk_cond_resid_d4_seqx_r8_d35ede'

def setup_inputs(seed: int=0):
    np.random.seed(seed)
    _w = jnp.asarray

    def _rec_inputs():
        import jax
        import jax.numpy as jnp
        _rk = jax.random.key(seed)
        x = -0.0005207 + 1.001 * jax.random.normal(jax.random.fold_in(_rk, 1), (32, 128, 128), jnp.float32)
        _lenS = 128 - jax.random.randint(jax.random.fold_in(_rk, 7), (32,), 0, max(1, 128 // 4) + 1, jnp.int32)
        _lenS2 = 128 - jax.random.randint(jax.random.fold_in(_rk, 8), (32,), 0, max(1, 128 // 4) + 1, jnp.int32)
        fside_Bx8_0 = jax.random.uniform(jax.random.fold_in(_rk, 11), (32, 8), jnp.float32, 0.0, 0.556406)
        condB_sharedgateprob = jax.random.uniform(jax.random.fold_in(_rk, 12), (32,), jnp.float32, 0.0, 0.794948)
        itok_B_0_15 = jax.random.randint(jax.random.fold_in(_rk, 13), (32,), 0, 16, jnp.int32)
        itok_B_0_63 = jax.random.randint(jax.random.fold_in(_rk, 14), (32,), 0, 64, jnp.int32)
        itok_B_0_2 = jax.random.randint(jax.random.fold_in(_rk, 15), (32,), 0, 3, jnp.int32)
        return (x, fside_Bx8_0, condB_sharedgateprob, itok_B_0_15, itok_B_0_63, itok_B_0_2)
    x, fside_Bx8_0, condB_sharedgateprob, itok_B_0_15, itok_B_0_63, itok_B_0_2 = _rec_inputs()

    def _L0_cond_setup():
        import jax, jax.numpy as jnp
        import numpy as np
        E, B, S, D, F = (8, 2, 128, 128, 512)
        key = jax.random.key(seed)
        ks = jax.random.split(key, 9)
        sc_d = 1.0 / np.sqrt(D)
        sc_f = 1.0 / np.sqrt(F)
        hidden_states = jax.random.normal(ks[0], (B, S, D), dtype=jnp.float32)
        gating_probs = jax.nn.softmax(jax.random.normal(ks[1], (B, E), dtype=jnp.float32), axis=-1)
        shared_gate_prob = jax.nn.sigmoid(jax.random.normal(ks[2], (B, 1), dtype=jnp.float32))
        Wg = jax.random.normal(ks[3], (E, D, F), dtype=jnp.float32) * sc_d
        Wu = jax.random.normal(ks[4], (E, D, F), dtype=jnp.float32) * sc_d
        Wd = jax.random.normal(ks[5], (E, F, D), dtype=jnp.float32) * sc_f
        Sg = jax.random.normal(ks[6], (D, F), dtype=jnp.float32) * sc_d
        Su = jax.random.normal(ks[7], (D, F), dtype=jnp.float32) * sc_d
        Sd = jax.random.normal(ks[8], (F, D), dtype=jnp.float32) * sc_f
        return {'hidden_states': hidden_states, 'gating_probs': gating_probs, 'shared_gate_prob': shared_gate_prob, 'Wg': Wg, 'Wu': Wu, 'Wd': Wd, 'Sg': Sg, 'Su': Su, 'Sd': Sd}
    _L0_cond_all = _L0_cond_setup()
    _L0_cond_in = {k: v for k, v in _L0_cond_all.items() if k in ('Wg', 'Wu', 'Wd', 'Sg', 'Su', 'Sd')}
    del _L0_cond_all

    def _L1_cond_setup():
        import jax, jax.numpy as jnp
        import numpy as np
        B, N, DIM = (32, 128, 128)
        HID = 512
        PART = 32
        OUT = 128
        SHARED = OUT - PART
        E = 16
        key = jax.random.key(seed)
        ks = jax.random.split(key, 8)
        s = 0.02
        return {'x': jax.random.normal(ks[0], (B, N, DIM), dtype=jnp.float32), 'indices': jax.random.randint(ks[1], (B,), 0, E, dtype=jnp.int64), 'fc1_w': jax.random.normal(ks[2], (HID, DIM), dtype=jnp.float32) * s, 'fc1_b': jnp.zeros((HID,), dtype=jnp.float32), 'fc2_w': jax.random.normal(ks[3], (SHARED, HID), dtype=jnp.float32) * s, 'fc2_b': jnp.zeros((SHARED,), dtype=jnp.float32), 'experts_w': jax.random.normal(ks[4], (E, PART, HID), dtype=jnp.float32) * s, 'experts_b': jnp.zeros((E, PART), dtype=jnp.float32)}
    _L1_cond_all = _L1_cond_setup()
    _L1_cond_in = {k: v for k, v in _L1_cond_all.items() if k in ('fc1_w', 'fc1_b', 'fc2_w', 'fc2_b', 'experts_w', 'experts_b')}
    del _L1_cond_all

    def _L2_cond_setup():
        import jax, jax.numpy as jnp
        import numpy as np
        NUM_CATEGORIES = 64
        INPUT_DIM = 128
        HIDDEN_DIM = 128
        B = 32
        S = 64
        key = jax.random.key(seed)
        kx, kc, kw = jax.random.split(key, 3)
        x = jax.random.normal(kx, (B, S, INPUT_DIM), dtype=jnp.float32)
        cat_ids = jax.random.randint(kc, (B,), 0, NUM_CATEGORIES, dtype=jnp.int32)
        W = 0.02 * jax.random.normal(kw, (NUM_CATEGORIES, INPUT_DIM, HIDDEN_DIM), dtype=jnp.float32)
        b = jnp.zeros((NUM_CATEGORIES, HIDDEN_DIM), dtype=jnp.float32)
        return {'x': x, 'cat_ids': cat_ids, 'W': W, 'b': b}
    _L2_cond_all = _L2_cond_setup()
    _L2_cond_in = {k: v for k, v in _L2_cond_all.items() if k in ('W', 'b')}
    del _L2_cond_all

    def _L3_cond_setup():
        import jax, jax.numpy as jnp
        import numpy as np
        D_MODEL = 128
        D_FF = 512
        N_EXPERTS = 5
        BATCH = 8
        SEQ = 256

        def _gated_ffn(x, wi0, wi1, wo):
            g = jax.nn.gelu(x @ wi0, approximate=True)
            l = x @ wi1
            return g * l @ wo
        key = jax.random.key(seed)
        ks = jax.random.split(key, 12)
        s = 0.02
        inp = {'hidden_states': jax.random.normal(ks[0], (BATCH, SEQ, D_MODEL), jnp.float32), 'type_label': jax.random.randint(ks[1], (BATCH,), 0, N_EXPERTS, jnp.int32), 'Wi0': jax.random.normal(ks[2], (N_EXPERTS, D_MODEL, D_FF), jnp.float32) * s, 'Wi1': jax.random.normal(ks[3], (N_EXPERTS, D_MODEL, D_FF), jnp.float32) * s, 'Wo': jax.random.normal(ks[4], (N_EXPERTS, D_FF, D_MODEL), jnp.float32) * s, 'sWi0': jax.random.normal(ks[5], (D_MODEL, D_FF), jnp.float32) * s, 'sWi1': jax.random.normal(ks[6], (D_MODEL, D_FF), jnp.float32) * s, 'sWo': jax.random.normal(ks[7], (D_FF, D_MODEL), jnp.float32) * s, 'g0': jax.random.normal(ks[8], (2 * D_MODEL, D_MODEL), jnp.float32) * s, 'g1': jax.random.normal(ks[9], (D_MODEL, 2), jnp.float32) * s}
        return inp
    _L3_cond_all = _L3_cond_setup()
    _L3_cond_in = {k: v for k, v in _L3_cond_all.items() if k in ('Wi0', 'Wi1', 'Wo', 'sWi0', 'sWi1', 'sWo', 'g0', 'g1')}
    del _L3_cond_all
    return {'x': x, 'fside_Bx8_0': fside_Bx8_0, 'condB_sharedgateprob': condB_sharedgateprob, 'itok_B_0_15': itok_B_0_15, 'itok_B_0_63': itok_B_0_63, 'itok_B_0_2': itok_B_0_2, 'L0_cond_Wg': _L0_cond_in['Wg'], 'L0_cond_Wu': _L0_cond_in['Wu'], 'L0_cond_Wd': _L0_cond_in['Wd'], 'L0_cond_Sg': _L0_cond_in['Sg'], 'L0_cond_Su': _L0_cond_in['Su'], 'L0_cond_Sd': _L0_cond_in['Sd'], 'L1_cond_fc1_w': _L1_cond_in['fc1_w'], 'L1_cond_fc1_b': _L1_cond_in['fc1_b'], 'L1_cond_fc2_w': _L1_cond_in['fc2_w'], 'L1_cond_fc2_b': _L1_cond_in['fc2_b'], 'L1_cond_experts_w': _L1_cond_in['experts_w'], 'L1_cond_experts_b': _L1_cond_in['experts_b'], 'L2_cond_W': _L2_cond_in['W'], 'L2_cond_b': _L2_cond_in['b'], 'L3_cond_Wi0': _L3_cond_in['Wi0'], 'L3_cond_Wi1': _L3_cond_in['Wi1'], 'L3_cond_Wo': _L3_cond_in['Wo'], 'L3_cond_sWi0': _L3_cond_in['sWi0'], 'L3_cond_sWi1': _L3_cond_in['sWi1'], 'L3_cond_sWo': _L3_cond_in['sWo'], 'L3_cond_g0': _L3_cond_in['g0'], 'L3_cond_g1': _L3_cond_in['g1']}

def reference(x, fside_Bx8_0, condB_sharedgateprob, itok_B_0_15, itok_B_0_63, itok_B_0_2, L0_cond_Wg, L0_cond_Wu, L0_cond_Wd, L0_cond_Sg, L0_cond_Su, L0_cond_Sd, L1_cond_fc1_w, L1_cond_fc1_b, L1_cond_fc2_w, L1_cond_fc2_b, L1_cond_experts_w, L1_cond_experts_b, L2_cond_W, L2_cond_b, L3_cond_Wi0, L3_cond_Wi1, L3_cond_Wo, L3_cond_sWi0, L3_cond_sWi1, L3_cond_sWo, L3_cond_g0, L3_cond_g1):
    import jax
    import jax.numpy as jnp

    def _L0_cond_ref(hidden_states, gating_probs, shared_gate_prob, Wg, Wu, Wd, Sg, Su, Sd):
        import jax, jax.numpy as jnp
        import numpy as np
        E, B, S, D, F = (8, 2, 128, 128, 512)
        h = hidden_states
        g = jnp.einsum('bsd,edf->ebsf', h, Wg)
        u = jnp.einsum('bsd,edf->ebsf', h, Wu)
        expert_outs = jnp.einsum('ebsf,efd->ebsd', jax.nn.silu(g) * u, Wd)
        expert_output = jnp.einsum('be,ebsd->bsd', gating_probs, expert_outs)
        shared = jnp.einsum('bsf,fd->bsd', jax.nn.silu(h @ Sg) * (h @ Su), Sd)
        sg = shared_gate_prob[:, :, None]
        return (1.0 - sg) * expert_output + sg * shared

    def _L1_cond_ref(x, indices, fc1_w, fc1_b, fc2_w, fc2_b, experts_w, experts_b):
        import jax, jax.numpy as jnp
        import numpy as np
        B, N, DIM = (32, 128, 128)
        HID = 512
        PART = 32
        OUT = 128
        SHARED = OUT - PART
        E = 16
        h = jax.nn.gelu(jnp.einsum('bnd,hd->bnh', x, fc1_w) + fc1_b, approximate=False)
        shared = jnp.einsum('bnh,sh->bns', h, fc2_w) + fc2_b
        We = experts_w[indices]
        be = experts_b[indices]
        expert_x = jnp.einsum('bnh,bph->bnp', h, We) + be[:, None, :]
        return jnp.concatenate([shared, expert_x], axis=-1)

    def _L2_cond_ref(x, cat_ids, W, b):
        import jax, jax.numpy as jnp
        import numpy as np
        NUM_CATEGORIES = 64
        INPUT_DIM = 128
        HIDDEN_DIM = 128
        B = 32
        S = 64
        selected_W = W[cat_ids]
        selected_b = b[cat_ids]
        out = jnp.einsum('bsd,bdh->bsh', x, selected_W) + selected_b[:, None, :]
        return out

    def _L3_cond_ref(hidden_states, type_label, Wi0, Wi1, Wo, sWi0, sWi1, sWo, g0, g1):
        import jax, jax.numpy as jnp
        import numpy as np
        D_MODEL = 128
        D_FF = 512
        N_EXPERTS = 5
        BATCH = 8
        SEQ = 256

        def _gated_ffn(x, wi0, wi1, wo):
            g = jax.nn.gelu(x @ wi0, approximate=True)
            l = x @ wi1
            return g * l @ wo
        share_out = _gated_ffn(hidden_states, sWi0, sWi1, sWo)
        wi0 = Wi0[type_label]
        wi1 = Wi1[type_label]
        wo = Wo[type_label]
        hg = jax.nn.gelu(jnp.einsum('bsd,bdf->bsf', hidden_states, wi0), approximate=True)
        hl = jnp.einsum('bsd,bdf->bsf', hidden_states, wi1)
        expert_out = jnp.einsum('bsf,bfd->bsd', hg * hl, wo)
        gate_in = jnp.concatenate([expert_out[:, 0], share_out[:, 0]], axis=-1)
        weights = jax.nn.softmax(jax.nn.relu(gate_in @ g0) @ g1, axis=-1)
        w0 = weights[:, 0][:, None, None]
        w1 = weights[:, 1][:, None, None]
        return expert_out * w0 + share_out * w1
    x = x + _L0_cond_ref(x, fside_Bx8_0, condB_sharedgateprob[:, None], L0_cond_Wg, L0_cond_Wu, L0_cond_Wd, L0_cond_Sg, L0_cond_Su, L0_cond_Sd)
    x = x + _L1_cond_ref(x, itok_B_0_15, L1_cond_fc1_w, L1_cond_fc1_b, L1_cond_fc2_w, L1_cond_fc2_b, L1_cond_experts_w, L1_cond_experts_b)
    x = x + _L2_cond_ref(x, itok_B_0_63, L2_cond_W, L2_cond_b)
    x = x + _L3_cond_ref(x, itok_B_0_2, L3_cond_Wi0, L3_cond_Wi1, L3_cond_Wo, L3_cond_sWi0, L3_cond_sWi1, L3_cond_sWo, L3_cond_g0, L3_cond_g1)
    return x

_drawn_inputs = setup_inputs


def setup_inputs(seed=0):
    import zlib

    import numpy as np

    out = dict(_drawn_inputs(seed))
    spreads = {'L1_cond_fc1_b': (0.0, 0.411),
     'L1_cond_fc2_b': (0.0, 0.1),
     'L1_cond_experts_b': (0.0, 0.1),
     'L2_cond_b': (0.0, 0.1)}
    factors = {'L3_cond_Wi0': 8.0,
     'L3_cond_Wi1': 8.0,
     'L3_cond_Wo': 8.0,
     'L3_cond_sWi0': 8.0,
     'L3_cond_sWi1': 7.995,
     'L3_cond_sWo': 7.971,
     'L3_cond_g0': 8.0,
     'L3_cond_g1': 8.0}
    for name, (base, spread) in spreads.items():
        noise = np.random.default_rng([zlib.crc32(name.encode()), seed]).standard_normal(out[name].shape)
        drawn = base * np.exp(spread * noise) if base else spread * noise
        out[name] = jnp.asarray(drawn.astype(out[name].dtype))
    for name, factor in factors.items():
        out[name] = (out[name] * factor).astype(out[name].dtype)
    return out
```

```python
from contextlib import ExitStack

import concourse.bass as bass
from concourse import mybir

F32 = mybir.dt.float32
F32R = mybir.dt.float32r
I32 = mybir.dt.int32
ALU = mybir.AluOpType
ACT = mybir.ActivationFunctionType
AX = mybir.AxisListType

P = 128
B = 32
GB = 4
GT = GB * P
NG = B // GB
NPAIR = NG // 2
FC = 4
F = FC * P
NE = 8
ROUNDS = NE + 1
E1 = 16
PART = 32
SHARED = P - PART
E2 = 64
E3 = 5
WSET = 3 * F
TILES = NG * FC

SET_AT = [2 * WSET, 0]
RING_AT = 4 * WSET
EXP_AT = 2 * WSET
EXP_STEP = 4 * F
RBUF = RING_AT + 2 * FC * 2 * GT


def reach(eng, sem, value):
    if isinstance(value, int) and value <= 0:
        return
    eng.wait_ge(sem, value)


def build_kernel(nc, x, fside, sgate, idx1, idx2, idx3, Wg, Wu, Wd, Sg, Su, Sd,
                 fc1_w, fc1_b, fc2_w, fc2_b, ex_w, ex_b, W2, b2,
                 Wi0, Wi1, Wo, sWi0, sWi1, sWo, g0, g1, out):
    with ExitStack() as ctx:
        def sb(name, shape, dt=F32):
            return ctx.enter_context(nc.sbuf_tensor(name, shape, dt))

        def bank(name):
            return ctx.enter_context(nc.psum_tensor(name, [P, GT], F32))

        def sem(name):
            return ctx.enter_context(nc.semaphore(name))

        psG = [bank("psG0"), bank("psG1")]
        psU = [bank("psU0"), bank("psU1")]
        psY = [bank("psY0"), bank("psY1")]
        psX = [bank("psX0"), bank("psX1")]

        xT = sb("xT", [P, B * P])
        xhi = sb("xhi", [P, B * P], F32R)
        xlo = sb("xlo", [P, B * P], F32R)
        rbuf = sb("rbuf", [P, RBUF], F32R)
        raw = sb("raw", [P, 2, WSET])
        act = sb("act", [P, 2, GT])
        hid = sb("hid", [P, 4, GT])
        h1 = sb("h1", [P, 2, FC, GT])
        ident = sb("ident", [P, P])
        gates = sb("gates", [P, ROUNDS * B])
        fs = sb("fs", [P, B * NE])
        omg = sb("omg", [P, B])
        fc1hi = sb("fc1hi", [P, F], F32R)
        fc1lo = sb("fc1lo", [P, F], F32R)
        fc1T = sb("fc1T", [P, F])
        fc1b = sb("fc1b", [P, FC])
        exT = sb("exT", [P, E1, FC, PART])
        w2 = sb("w2", [P, 2, GB, FC, P])
        bias1 = sb("bias1", [P, B])
        bias2 = sb("bias2", [P, B])
        idxs = sb("idxs", [1, 3, B], I32)
        hot = sb("hot", [E2, 2, B])
        wcat = sb("wcat", [P, 2, GB, P])
        woe = sb("woe", [P, E3, FC, P])
        g1b = sb("g1b", [P, 2, P])
        g0s = sb("g0s", [P, 2, P])
        xs_hi = sb("xs_hi", [P, 2, GT], F32R)
        xs_lo = sb("xs_lo", [P, 2, GT], F32R)
        idxb = sb("idxb", [E2, 2, B], I32)
        idxf = sb("idxf", [E2, 2, B])
        row_id = sb("row_id", [E2, 1], I32)
        row_f = sb("row_f", [E2, 1])
        table1 = sb("table1", [E1, P])
        table2 = sb("table2", [E2, P])
        e0r = sb("e0r", [2 * GB, P])
        g1s = sb("g1s", [P, 2])
        gE = sb("gE", [P, 2 * GB])
        gS = sb("gS", [P, 2 * GB])
        ghid = sb("ghid", [P, 2 * GB])
        glog = sb("glog", [P, 2, 2 * GB])
        gmax = sb("gmax", [P, 2 * GB])
        gdiff = sb("gdiff", [P, 2, 2 * GB])
        gexp = sb("gexp", [P, 2, 2 * GB])
        gsum = sb("gsum", [P, 2 * GB])
        grec = sb("grec", [P, 2 * GB])
        gw = sb("gw", [P, 2, 2 * GB])

        h1f = h1[:, :, :, :].rearrange("p a c n -> p (a c n)")
        xtok = h1f.rearrange("p (b d) -> p b d", b=B)
        hT = h1f[:, 0:2 * F].rearrange("p (a n) -> p a n", a=2)
        esb = h1f[:, 2 * F:4 * F].rearrange("p (a j n) -> p a j n", a=2, j=GB)
        ssb = h1f[:, 4 * F:6 * F].rearrange("p (a j n) -> p a j n", a=2, j=GB)
        osb = h1f[:, 6 * F:8 * F].rearrange("p (a j n) -> p a j n", a=2, j=GB)
        w2f = w2[:, :, :, :, :].rearrange("p a j c n -> p (a j c n)")
        z = w2f[:, 0:2 * GT].rearrange("p (a j n) -> p a j n", a=2, j=GB)
        exraw = woe[:, :, :, :].rearrange("p e c n -> p (e c n)")[:, 0:4 * F].rearrange("p (r f) -> p r f", r=4)
        fc2raw = wcat[0:SHARED, 0, :, :].rearrange("p j n -> p (j n)")
        fc1raw = wcat[:, 1, :, :]

        def wset(par, lo, q, c):
            at = SET_AT[par] + lo * WSET + q * F + c * P
            return rbuf[:, at:at + P]

        def shid(c, lo):
            return (xlo if lo else xhi)[:, c * GT:(c + 1) * GT]

        def ring(half, c, lo):
            at = RING_AT + (half * FC + c) * 2 * GT + lo * GT
            return rbuf[:, at:at + GT]

        x_in = [sem(f"x_in{g}") for g in range(NG)]
        small_in, idx_in, l1w_in, g_in = sem("small_in"), sem("idx_in"), sem("l1w_in"), sem("g_in")
        raw_in = [sem("raw_in0"), sem("raw_in1")]
        cat_in = [sem("cat_in0"), sem("cat_in1")]
        wo_in, e0_in, out_sem = sem("wo_in"), sem("e0_in"), [sem("out_sem0"), sem("out_sem1")]
        ident_ok, hot_ok = sem("ident_ok"), sem("hot_ok")
        xt_ready, xt_done, xhi_done, xlo_done = sem("xt_ready"), sem("xt_done"), sem("xhi_done"), sem("xlo_done")
        gates_ok, g1b_ok = sem("gates_ok"), sem("g1b_ok")
        tr_ready, tr_done, fc1hi_ok, fc1lo_ok, fc2_ok = (sem("tr_ready"), sem("tr_done"), sem("fc1hi_ok"),
                                                         sem("fc1lo_ok"), sem("fc2_ok"))
        bias_ready, bias_ok = sem("bias_ready"), sem("bias_ok")
        whi_done, wlo_done = sem("whi_done"), sem("wlo_done")
        g_ready, u_ready, d_done = sem("g_ready"), sem("u_ready"), sem("d_done")
        silu_done, mul_done, hi_done, lo_done, y_added = (sem("silu_done"), sem("mul_done"), sem("hi_done"),
                                                          sem("lo_done"), sem("y_added"))
        fc_ready, gelu_done, l1_ready, l2_ready = sem("fc_ready"), sem("gelu_done"), sem("l1_ready"), sem("l2_ready")
        x1hi, x1lo, x2_done, x3_done, w2_ready = (sem("x1hi"), sem("x1lo"), sem("x2_done"), sem("x3_done"),
                                                  sem("w2_ready"))
        p_in = [sem("p_in0"), sem("p_in1")]
        phi_done, plo_done = sem("phi_done"), sem("plo_done")
        xshi, xslo = sem("xshi"), sem("xslo")
        g3, u3, gelu3, mul3 = sem("g3"), sem("u3"), sem("gelu3"), sem("mul3")
        shi, slo, s_ready, s_out = sem("shi"), sem("slo"), sem("s_ready"), sem("s_out")
        t_ready, t_out, e_done, e_ready, e_out = (sem("t_ready"), sem("t_out"), sem("e_done"), sem("e_ready"),
                                                  sem("e_out"))
        gate_pe, gate_dve, gate_exp, z_done, z_ready, o_done = (sem("gate_pe"), sem("gate_dve"), sem("gate_exp"),
                                                                sem("z_done"), sem("z_ready"), sem("o_done"))

        TL0 = ROUNDS * TILES

        block = ctx.enter_context(nc.Block())

        @block.sync
        def _(sp):
            def load_raw(par, gate, up, down, free):
                if free is not None:
                    sp.wait_ge(wlo_done, free)
                for q, w in ((0, gate), (1, up)):
                    sp.dma_start(raw[:, par, q * F:(q + 1) * F], w).then_inc(raw_in[par], 16)
                sp.dma_start(raw[:, par, 2 * F:3 * F].rearrange("p (c d) -> p c d", c=FC),
                             down.rearrange("(c p) d -> p c d", p=P)).then_inc(raw_in[par], 16)

            for g in range(2):
                sp.dma_start(xtok[:, g * GB:(g + 1) * GB, :],
                             x[g * GB:(g + 1) * GB].rearrange("b n d -> n b d")).then_inc(x_in[g], 16)
            load_raw(0, Sg, Su, Sd, None)
            for g in range(2, NG):
                sp.dma_start(xtok[:, g * GB:(g + 1) * GB, :],
                             x[g * GB:(g + 1) * GB].rearrange("b n d -> n b d")).then_inc(x_in[g], 16)
            load_raw(1, Wg[0], Wu[0], Wd[0], None)
            sp.dma_start(exraw, ex_w.rearrange("e p f -> (e p) f").rearrange("(r q) f -> q r f", q=P)) \
                .then_inc(l1w_in, 16)
            sp.dma_start(fc2raw, fc2_w).then_inc(l1w_in, 16)
            sp.dma_start(fc1raw, fc1_w.rearrange("(c q) d -> q c d", q=P)).then_inc(l1w_in, 16)
            sp.dma_start(g0s[:, :, :], g0.rearrange("(a p) d -> p a d", p=P)).then_inc(g_in, 16)
            with sp.Fori(1, NPAIR) as p:
                load_raw(0, Wg[bass.ds(2 * p - 1, 1)].rearrange("a d f -> (a d) f"),
                         Wu[bass.ds(2 * p - 1, 1)].rearrange("a d f -> (a d) f"),
                         Wd[bass.ds(2 * p - 1, 1)].rearrange("a d f -> (a d) f"), 6 * p - 3)
                load_raw(1, Wg[bass.ds(2 * p, 1)].rearrange("a d f -> (a d) f"),
                         Wu[bass.ds(2 * p, 1)].rearrange("a d f -> (a d) f"),
                         Wd[bass.ds(2 * p, 1)].rearrange("a d f -> (a d) f"), 6 * p)
            load_raw(0, Wg[NE - 1], Wu[NE - 1], Wd[NE - 1], 3 * (ROUNDS - 2))
            load_raw(1, sWi0, sWi1, sWo, 3 * (ROUNDS - 1))
            sp.wait_ge(tr_done, 6)
            for e in range(E3):
                sp.dma_start(woe[:, e, :, :], Wo[e].rearrange("(c p) d -> p c d", p=P)).then_inc(wo_in, 16)

            def load_cat(b, half, j):
                n = sp.value_load(idxs[0:1, 1, b], min_val=0, max_val=E2 - 1)
                sp.dma_start(wcat[:, half, j, :], W2[bass.ds(n, 1)].rearrange("a d h -> (a d) h")) \
                    .then_inc(cat_in[half], 16)

            def load_piece(half, e, free):
                if free is not None:
                    sp.wait_ge(plo_done, free)
                w = (Wi0, Wi1)[half]
                src = w[e] if isinstance(e, int) else w[bass.ds(e, 1)].rearrange("a d f -> (a d) f")
                sp.dma_start(raw[:, half, 0:F], src).then_inc(p_in[half], 16)

            sp.wait_ge(idx_in, 48)
            for half in range(2):
                for j in range(GB):
                    load_cat(bass.ds(half * GB + j, 1), half, j)
            sp.wait_ge(wlo_done, 3 * (ROUNDS + 1))
            for half in range(2):
                load_piece(half, 0, None)
            with sp.Fori(1, NPAIR) as p:
                for half in range(2):
                    load_piece(half, p, 2 * p + half - 1)
                    sp.wait_ge(l2_ready, 2 * p + half - 1)
                    for j in range(GB):
                        load_cat(bass.ds(8 * p + (half * GB + j), 1), half, j)
            for half in range(2):
                load_piece(half, E3 - 1, 2 * (E3 - 1) + half - 1)

            def finish_pair(p):
                sp.wait_ge(e_out, 2 * p + 2)
                sp.dma_start(e0r[:, :], esb[0:1, :, :, :].rearrange("o a j n -> o (a j) n")).then_inc(e0_in, 16)
                for half in range(2):
                    sp.wait_ge(o_done, 2 * GB * p + GB * (half + 1))
                    b0 = 8 * p + half * GB
                    dst = out[b0:b0 + GB] if isinstance(p, int) else out[bass.ds(b0, GB)]
                    sp.dma_start(dst.rearrange("b n d -> n b d"), osb[:, half, :, :]).then_inc(out_sem[half], 16)

            with sp.Fori(0, NPAIR) as p:
                finish_pair(p)
            for half in range(2):
                sp.wait_ge(out_sem[half], 16 * NPAIR)

        @block.gpsimd
        def _(pool):
            pool.memset(ident[:, :], 0.0).then_inc(ident_ok, 1)
            pool.wait_ge(ident_ok, 1)
            pool.affine_select(out=ident[:, :], in_=ident[:, :], compare_op=ALU.not_equal, fill=1.0, base=0,
                               pattern=[[-1, P]], channel_multiplier=1).then_inc(ident_ok, 1)
            pool.iota(row_id[:, :], pattern=[[0, 1]], base=0, channel_multiplier=1).then_inc(hot_ok, 1)
            pool.wait_ge(tr_done, 5)
            for s in range(1, 2 * GB):
                pool.tensor_copy(w2[:, s // GB, s % GB, :, 0:SHARED], w2[:, 0, 0, :, 0:SHARED]).then_inc(fc2_ok, 1)
            pool.wait_ge(tr_done, 6)
            pool.wait_ge(idx_in, 48)

            def expert_columns(b, half, j, free):
                n = pool.value_load(idxs[0:1, 0, b], min_val=0, max_val=E1 - 1)
                if free is not None:
                    pool.wait_ge(l1_ready, free)
                pool.tensor_copy(w2[:, half, j, :, SHARED:P],
                                 exT[:, bass.ds(n, 1), :, :].rearrange("p a c n -> p (a c) n")).then_inc(w2_ready, 1)

            for s in range(2 * GB):
                expert_columns(bass.ds(s, 1), s // GB, s % GB, None)
            with pool.Fori(1, NPAIR) as p:
                for s in range(2 * GB):
                    expert_columns(bass.ds(8 * p + s, 1), s // GB, s % GB, 8 * p + (s - 7))

        @block.scalar
        def _(sc):
            sc.dma_start(gates[:, 0:B], sgate.partition_broadcast(P)).then_inc(small_in, 16)
            sc.dma_start(fs[:, :], fside.rearrange("b e -> (b e)").partition_broadcast(P)).then_inc(small_in, 16)
            sc.dma_start(idxs[0:1, 0, :], idx1.rearrange("(a b) -> a b", a=1)).then_inc(idx_in, 16)
            sc.dma_start(idxs[0:1, 1, :], idx2.rearrange("(a b) -> a b", a=1)).then_inc(idx_in, 16)
            sc.dma_start(idxs[0:1, 2, :], idx3.rearrange("(a b) -> a b", a=1)).then_inc(idx_in, 16)
            with nc.allow_non_contiguous_dma(reason="128 x 4 and 128 x 2 numbers"):
                sc.dma_start(fc1b[:, :], fc1_b.rearrange("(c p) -> p c", p=P)).then_inc(g_in, 16)
                sc.dma_start(g1s[:, :], g1).then_inc(g_in, 16)
            sc.dma_start(idxb[:, 0, :], idx1.partition_broadcast(E2)).then_inc(g_in, 16)
            sc.dma_start(idxb[:, 1, :], idx2.partition_broadcast(E2)).then_inc(g_in, 16)
            sc.dma_start(table1[:, SHARED:P], ex_b).then_inc(g_in, 16)
            sc.dma_start(table1[:, 0:SHARED], fc2_b.partition_broadcast(E1)).then_inc(g_in, 16)
            sc.dma_start(table2[:, :], b2).then_inc(g_in, 16)

            for q in range(3):
                sc.wait_ge(raw_in[0], 48)
                sc.activation(rbuf[:, SET_AT[0] + q * F:SET_AT[0] + (q + 1) * F], raw[:, 0, q * F:(q + 1) * F],
                              ACT.Copy).then_inc(whi_done, 1)
                if q < 2:
                    sc.wait_ge(xt_done, q + 1)
                    sc.activation(xhi[:, q * GT:(q + 1) * GT], xT[:, q * GT:(q + 1) * GT], ACT.Copy) \
                        .then_inc(xhi_done, 1)
            for g in range(2, NG):
                sc.wait_ge(xt_done, g + 1)
                sc.activation(xhi[:, g * GT:(g + 1) * GT], xT[:, g * GT:(g + 1) * GT], ACT.Copy) \
                    .then_inc(xhi_done, 1)

            def slot(T, half, c, gu=True, hi=True):
                if gu:
                    sc.wait_ge(g_ready, T + 1)
                    reach(sc, mul_done, T - 1)
                    sc.activation(act[:, c % 2, :], psG[c % 2][:, :], ACT.Silu).then_inc(silu_done, 1)
                if hi:
                    sc.wait_ge(mul_done, T)
                    reach(sc, d_done, T - 8)
                    h, k = (half, c - 1) if c else (1 - half, FC - 1)
                    sc.activation(ring(h, k, 0), hid[:, k, :], ACT.Copy).then_inc(hi_done, 1)

            def pair(T0, head=False, split=None):
                for half in range(2):
                    for c in range(FC):
                        slot(T0 + (4 * half + c), half, c, hi=not (head and half + c == 0))
                        if split and half == 0 and c == 1:
                            par, gp, loaded, over = split
                            sc.wait_ge(raw_in[par], loaded)
                            reach(sc, d_done, over)
                            sc.activation(rbuf[:, bass.ds((gp - 1) * F + SET_AT[par], F)],
                                          raw[:, par, bass.ds((gp - 1) * F, F)], ACT.Copy).then_inc(whi_done, 1)

            pair(0, head=True)
            with sc.Fori(1, NPAIR) as gp:
                pair(8 * gp, split=(1, gp, 48, 0))
            sc.wait_ge(tr_done, 6)
            sc.activation(fc1hi[:, :], fc1T[:, :], ACT.Copy).then_inc(fc1hi_ok, 1)
            with sc.Fori(0, NE // 2) as p:
                for k in range(2):
                    pair(64 * p + 32 * (k + 1))
                    with sc.Fori(1, NPAIR) as gp:
                        pair(64 * p + 8 * gp + 32 * (k + 1),
                             split=(k, gp, 48 * p + 96, 64 * p + 32 * (k + 1)))
            slot(TL0, 0, 0, gu=False)

            def split_x1(g):
                sc.wait_ge(y_added, 4 * g + (TL0 - TILES + 4))
                sc.wait_ge(u_ready, 4 * g + (TL0 - TILES + 4))
                sc.activation(xhi[:, bass.ds(g * GT, GT)], xT[:, bass.ds(g * GT, GT)], ACT.Copy).then_inc(x1hi, 1)

            def l1_slot(g, half, e):
                if not isinstance(g, int) or g < NG:
                    for c in range(FC):
                        sc.wait_ge(fc_ready, 4 * g + (c + 1))
                        if c == 0:
                            reach(sc, l1_ready, 4 * g - 4)
                        sc.activation(h1[:, half, c, :], psG[c % 2][:, :], ACT.Gelu, bias=fc1b[:, c:c + 1]) \
                            .then_inc(gelu_done, 1)
                        if c == 1 and (not isinstance(g, int) or g + 1 < NG):
                            split_x1(g + 1)
                if e is not None:
                    sc.wait_ge(p_in[half], 16 * e + 16)
                    sc.wait_ge(d_done, TL0)
                    at = EXP_AT + half * 2 * F
                    sc.activation(rbuf[:, bass.ds(e * EXP_STEP + at, F)], raw[:, half, 0:F], ACT.Copy) \
                        .then_inc(phi_done, 1)

            sc.wait_ge(g_in, 16 * 8)
            split_x1(0)
            for half in range(2):
                l1_slot(half, half, 0)
            with sc.Fori(1, NPAIR - 1) as p:
                for half in range(2):
                    l1_slot(2 * p + half, half, p)
            for half in range(2):
                l1_slot(NG - 2 + half, half, NPAIR - 1)
            for half in range(2):
                l1_slot(NG + half, half, E3 - 1)

            def split_x3(g, half):
                sc.wait_ge(x3_done, 4 * g + 4)
                reach(sc, u3, 8 * g - 8)
                sc.activation(xs_hi[:, half, :], xT[:, bass.ds(g * GT, GT)], ACT.Copy).then_inc(xshi, 1)

            def l3_slot(g, half, first=False, last=False, stream=True, mix=None):
                for k in range(8):
                    K = 8 * g + k
                    if stream:
                        sc.wait_ge(g3, K + 1)
                        reach(sc, mul3, K - 1)
                        sc.activation(act[:, k % 2, :], psG[k % 2][:, :], ACT.Gelu_apprx_tanh).then_inc(gelu3, 1)
                        if k % 2 == 1:
                            q = 4 * g + (k - 1) // 2
                            sc.wait_ge(mul3, K)
                            reach(sc, d_done, q - 3 + TL0)
                            sc.activation(shid((k - 1) // 2, 0), hid[:, (k - 1) % 4, :], ACT.Copy).then_inc(shi, 1)
                    if k % 2 == 0 and (not first or k >= 4) and (stream or k < 4):
                        r = 4 * g + (k // 2 - 2)
                        sc.wait_ge(t_ready, r + 1)
                        reach(sc, e_done, r - 1)
                        sc.activation(hT[:, (k // 2) % 2, :], psX[0][:, :], ACT.Copy).then_inc(t_out, 1)
                    if k == 0 and mix is not None:
                        gate_exp_of(mix)
                    if k == 1 and not first:
                        sc.wait_ge(d_done, 4 * g + TL0)
                        reach(sc, z_done, 4 * g - 8)
                        sc.activation(ssb[:, 1 - half, :, :].rearrange("p j n -> p (j n)"), psY[0][:, :], ACT.Copy) \
                            .then_inc(s_out, 1)
                    if k == 4 and not first:
                        sc.wait_ge(e_done, 4 * g)
                        reach(sc, o_done, 4 * g - 8)
                        sc.activation(esb[:, 1 - half, :, :].rearrange("p j n -> p (j n)"), psY[1][:, :], ACT.Copy) \
                            .then_inc(e_out, 1)
                    if k == 6 and not last and stream:
                        split_x3(g + 1, 1 - half)

            def gate_exp_of(p):
                sc.wait_ge(gate_dve, 9 * p + 6)
                sc.activation(gexp[:, :, :], gdiff[:, :, :], ACT.Exp).then_inc(gate_exp, 1)

            split_x3(0, 0)
            l3_slot(0, 0, first=True)
            l3_slot(1, 1)
            with sc.Fori(1, NPAIR - 1) as p:
                l3_slot(2 * p, 0)
                l3_slot(2 * p + 1, 1, mix=p - 1)
            l3_slot(NG - 2, 0)
            l3_slot(NG - 1, 1, last=True, mix=NPAIR - 2)
            l3_slot(NG, 0, stream=False)
            gate_exp_of(NPAIR - 1)

        @block.vector
        def _(ve):
            def split_lo(dst, value, hi, done):
                ve.tensor_tensor(dst, value, hi.bitcast(F32), ALU.subtract).then_inc(done, 1)

            ve.wait_ge(small_in, 32)
            ve.tensor_scalar(omg[:, :], gates[:, 0:B], -1.0, 1.0, ALU.mult, ALU.add).then_inc(gates_ok, 1)
            ve.wait_ge(gates_ok, 1)
            ve.tensor_tensor(gates[:, B:ROUNDS * B].rearrange("p (e b) -> p e b", e=NE),
                             fs[:, :].rearrange("p (b e) -> p e b", e=NE),
                             omg[:, :].unsqueeze(1).to_broadcast([P, NE, B]), ALU.mult).then_inc(gates_ok, 1)

            def x_out(g):
                ve.wait_ge(xt_ready, g + 1)
                ve.tensor_copy(xT[:, g * GT:(g + 1) * GT], psX[g % 2][:, :]).then_inc(xt_done, 1)

            def x_lo(g):
                ve.wait_ge(xhi_done, g + 1)
                ve.wait_ge(xt_done, g + 1)
                split_lo(xlo[:, g * GT:(g + 1) * GT], xT[:, g * GT:(g + 1) * GT], xhi[:, g * GT:(g + 1) * GT],
                         xlo_done)

            for g in range(NG):
                x_out(g)
                if g < 3:
                    ve.wait_ge(whi_done, g + 1)
                    ve.wait_ge(raw_in[0], 48)
                    split_lo(rbuf[:, SET_AT[0] + WSET + g * F:SET_AT[0] + WSET + (g + 1) * F],
                             raw[:, 0, g * F:(g + 1) * F], rbuf[:, SET_AT[0] + g * F:SET_AT[0] + (g + 1) * F],
                             wlo_done)
                if g:
                    x_lo(g - 1)
            x_lo(NG - 1)

            def slot(T, half, c, gu=True, lo=True, add=None):
                if gu:
                    ve.wait_ge(silu_done, T + 1)
                    ve.wait_ge(u_ready, T + 1)
                    reach(ve, lo_done, T - 3)
                    ve.tensor_tensor(hid[:, c, :], act[:, c % 2, :], psU[c % 2][:, :], ALU.mult).then_inc(mul_done, 1)
                if lo:
                    ve.wait_ge(hi_done, T)
                    ve.wait_ge(mul_done, T)
                    reach(ve, d_done, T - 8)
                    h, k = (half, c - 1) if c else (1 - half, FC - 1)
                    split_lo(ring(h, k, 1), hid[:, k, :], ring(h, k, 0), lo_done)
                if add:
                    groups, col = add
                    ve.wait_ge(d_done, 4 * groups)
                    xb = xT[:, bass.ds(col, P)]
                    ve.scalar_tensor_tensor(out=xb, in0=psY[half][:, c * P:(c + 1) * P],
                                            scalar=gates[:, bass.ds(T - 8, 1)], in1=xb,
                                            op0=ALU.mult, op1=ALU.add).then_inc(y_added, 1)

            def pair(T0, G0, col, head=False, split=None):
                for half in range(2):
                    for c in range(FC):
                        at = 4 * half + c
                        slot(T0 + at, half, c, lo=not (head and at == 0),
                             add=None if head else (G0 + half - 1, col + at * P))
                        if split and half == 0 and c == 2:
                            par, gp, third = split
                            ve.wait_ge(whi_done, third)
                            split_lo(rbuf[:, bass.ds((gp - 1) * F + (SET_AT[par] + WSET), F)],
                                     raw[:, par, bass.ds((gp - 1) * F, F)],
                                     rbuf[:, bass.ds((gp - 1) * F + SET_AT[par], F)], wlo_done)

            pair(0, 0, 0, head=True)
            with ve.Fori(1, NPAIR) as gp:
                pair(8 * gp, 2 * gp, 8 * P * gp - 8 * P, split=(1, gp, gp + 3))

            for i in range(4):
                ve.wait_ge(tr_ready, i + 1)
                ve.tensor_copy(exT[:, 4 * i:4 * i + 4, :, :].rearrange("p e c n -> p c e n"),
                               psX[i % 2][:, :].rearrange("p (c e n) -> p c e n", c=FC, e=4)).then_inc(tr_done, 1)
            ve.wait_ge(tr_ready, 5)
            ve.tensor_copy(w2[:, 0, 0, :, 0:SHARED],
                           psX[0][:, 0:FC * SHARED].rearrange("p (c n) -> p c n", c=FC)).then_inc(tr_done, 1)
            ve.wait_ge(tr_ready, 6)
            ve.tensor_copy(fc1T[:, :], psX[1][:, :]).then_inc(tr_done, 1)
            ve.wait_ge(hot_ok, 1)
            ve.wait_ge(g_in, 16 * 8)
            ve.tensor_copy(row_f[:, :], row_id[:, :]).then_inc(hot_ok, 1)
            ve.tensor_copy(idxf[:, :, :], idxb[:, :, :]).then_inc(hot_ok, 1)
            ve.wait_ge(hot_ok, 3)
            ve.tensor_scalar(hot[:, :, :], idxf[:, :, :], row_f[:, 0:1], None, ALU.is_equal).then_inc(hot_ok, 1)
            ve.wait_ge(bias_ready, 2)
            ve.tensor_copy(bias1[:, :], psX[0][:, 0:B]).then_inc(bias_ok, 1)
            ve.tensor_copy(bias2[:, :], psX[1][:, 0:B]).then_inc(bias_ok, 1)
            for a in range(2):
                ve.tensor_copy(g1b[:, a, :], g1s[:, a:a + 1].to_broadcast([P, P])).then_inc(g1b_ok, 1)
            ve.wait_ge(fc1hi_ok, 1)
            split_lo(fc1lo[:, :], fc1T[:, :], fc1hi[:, :], fc1lo_ok)

            with ve.Fori(0, NE // 2) as p:
                for k in range(2):
                    T0 = 64 * p + 32 * (k + 1)
                    G0 = 16 * p + 8 * (k + 1)
                    pair(T0, G0, 24 * P)
                    with ve.Fori(1, NPAIR) as gp:
                        pair(64 * p + 8 * gp + 32 * (k + 1), 16 * p + 2 * gp + 8 * (k + 1), 8 * P * gp - 8 * P,
                             split=(k, gp, 6 * p + gp + (6 + 3 * k)))
            slot(TL0, 0, 0, gu=False, add=(TL0 // FC - 1, 24 * P))
            for at in range(1, 8):
                slot(TL0 + at, at // 4, at % 4, gu=False, lo=False, add=(TL0 // FC + at // 4 - 1, (24 + at) * P))

            def x1_lo(g):
                ve.wait_ge(x1hi, g + 1)
                split_lo(xlo[:, bass.ds(g * GT, GT)], xT[:, bass.ds(g * GT, GT)], xhi[:, bass.ds(g * GT, GT)], x1lo)

            def residual(g, src, bias, done):
                for j in range(GB):
                    xb = xT[:, bass.ds(g * GT + j * P, P)]
                    ve.scalar_tensor_tensor(out=xb, in0=src[:, j * P:(j + 1) * P],
                                            scalar=bias[:, bass.ds(4 * g + j, 1)], in1=xb,
                                            op0=ALU.add, op1=ALU.add).then_inc(done, 1)

            def in_range(g, a, b):
                return not isinstance(g, int) or a <= g <= b

            def l1_slot(g, half, e):
                if in_range(g, 3, NG + 2):
                    ve.wait_ge(l2_ready, g - 2)
                    residual(g - 3, psX[1 - half], bias2, x3_done)
                if in_range(g, 0, NG - 2):
                    x1_lo(g + 1)
                if e is not None:
                    ve.wait_ge(phi_done, 2 * e + half + 1)
                    at = EXP_AT + half * 2 * F
                    split_lo(rbuf[:, bass.ds(e * EXP_STEP + (at + F), F)], raw[:, half, 0:F],
                             rbuf[:, bass.ds(e * EXP_STEP + at, F)], plo_done)
                if in_range(g, 1, NG):
                    ve.wait_ge(l1_ready, 4 * g)
                    residual(g - 1, psY[1 - half], bias1, x2_done)

            ve.wait_ge(bias_ok, 2)
            ve.wait_ge(y_added, TL0)
            x1_lo(0)
            for g in range(NG + 3):
                l1_slot(g, g % 2, g // 2 if g < 2 * E3 else None)

            def x3_lo(g, half):
                ve.wait_ge(xshi, g + 1)
                split_lo(xs_lo[:, half, :], xT[:, bass.ds(g * GT, GT)], xs_hi[:, half, :], xslo)

            def gate_step(op, done, n):
                ve.wait_ge(gate_dve, done)
                op().then_inc(gate_dve, 1)

            def gate_columns(p):
                ve.wait_ge(gate_pe, 3 * p + 1)
                ve.tensor_copy(gE[:, :], psX[1][:, 0:2 * GB]).then_inc(gate_dve, 1)
                ve.wait_ge(s_out, 2 * p + 2)
                ve.tensor_copy(gS[:, :], ssb[:, :, :, 0:1].rearrange("p a j n -> p (a j n)")).then_inc(gate_dve, 1)

            def gate_relu(p):
                ve.wait_ge(gate_pe, 3 * p + 2)
                ve.tensor_scalar(ghid[:, :], psX[1][:, 8:8 + 2 * GB], 0.0, None, ALU.max).then_inc(gate_dve, 1)

            def gate_max(p):
                ve.wait_ge(gate_pe, 3 * p + 3)
                ve.tensor_copy(glog[:, :, :], psX[1][:, 16:16 + 4 * GB].rearrange("p (a b) -> p a b", a=2)) \
                    .then_inc(gate_dve, 1)
                ve.wait_ge(gate_dve, 9 * p + 4)
                ve.tensor_tensor(gmax[:, :], glog[:, 0, :], glog[:, 1, :], ALU.max).then_inc(gate_dve, 1)
                ve.wait_ge(gate_dve, 9 * p + 5)
                ve.tensor_tensor(gdiff[:, :, :], glog[:, :, :], gmax[:, :].unsqueeze(1).to_broadcast([P, 2, 2 * GB]),
                                 ALU.subtract).then_inc(gate_dve, 1)

            def gate_weights(p):
                ve.wait_ge(gate_exp, p + 1)
                ve.tensor_tensor(gsum[:, :], gexp[:, 0, :], gexp[:, 1, :], ALU.add).then_inc(gate_dve, 1)
                ve.wait_ge(gate_dve, 9 * p + 7)
                ve.reciprocal(grec[:, :], gsum[:, :]).then_inc(gate_dve, 1)
                ve.wait_ge(gate_dve, 9 * p + 8)
                ve.tensor_tensor(gw[:, :, :], gexp[:, :, :], grec[:, :].unsqueeze(1).to_broadcast([P, 2, 2 * GB]),
                                 ALU.mult).then_inc(gate_dve, 1)
                ve.wait_ge(gate_dve, 9 * p + 9)

            def mix_shared(p, a):
                reach(ve, z_ready, 2 * p)
                for j in range(GB):
                    n = a * GB + j
                    ve.scalar_tensor_tensor(out=z[:, a, j, :], in0=ssb[:, a, j, :], scalar=gw[:, 1, n:n + 1],
                                            in1=xT[:, bass.ds(p * (2 * GT) + n * P, P)],
                                            op0=ALU.mult, op1=ALU.add).then_inc(z_done, 1)

            def mix_expert(p, a):
                ve.wait_ge(z_ready, 2 * p + a + 1)
                reach(ve, out_sem[a], 16 * p)
                for j in range(GB):
                    n = a * GB + j
                    ve.scalar_tensor_tensor(out=osb[:, a, j, :], in0=esb[:, a, j, :], scalar=gw[:, 0, n:n + 1],
                                            in1=psX[1][:, j * P:(j + 1) * P],
                                            op0=ALU.mult, op1=ALU.add).then_inc(o_done, 1)

            def mix(p, half, k):
                if (half, k) == (0, 6):
                    gate_columns(p)
                if (half, k) == (0, 7):
                    gate_relu(p)
                if (half, k) == (1, 0):
                    gate_max(p)
                if (half, k) == (1, 1):
                    gate_weights(p)
                    mix_shared(p, 0)
                    mix_shared(p, 1)
                if (half, k) == (1, 3):
                    mix_expert(p, 0)
                if (half, k) == (1, 5):
                    mix_expert(p, 1)

            def l3_slot(g, half, p=None):
                for k in range(8):
                    K = 8 * g + k
                    ve.wait_ge(gelu3, K + 1)
                    ve.wait_ge(u3, K + 1)
                    if k % 2 == 0:
                        reach(ve, slo, 4 * g + (k // 2 - 1))
                    else:
                        reach(ve, t_ready, 4 * g + (k // 2 - 1))
                    ve.tensor_tensor(hid[:, k % 4, :], act[:, k % 2, :], psU[k % 2][:, :], ALU.mult).then_inc(mul3, 1)
                    if k % 2 == 1:
                        ve.wait_ge(shi, 4 * g + (k // 2 + 1))
                        split_lo(shid(k // 2, 1), hid[:, (k - 1) % 4, :], shid(k // 2, 0), slo)
                    if p is not None:
                        mix(p, half, k)
                    if k == 7 and in_range(g, 0, NG - 2):
                        x3_lo(g + 1, 1 - half)

            x3_lo(0, 0)
            for half in range(2):
                l3_slot(half, half)
            with ve.Fori(1, NPAIR - 1) as p:
                for half in range(2):
                    l3_slot(2 * p + half, half, p - 1)
            for half in range(2):
                l3_slot(NG - 2 + half, half, NPAIR - 2)
            for half in range(2):
                for k in range(8):
                    mix(NPAIR - 1, half, k)

        @block.tensor
        def _(pe):
            def three(bank_, whi, wlo, mhi, mlo, start, stop):
                pe.matmul(bank_, whi, mhi, start=start, stop=False)
                pe.matmul(bank_, wlo, mhi, start=False, stop=False)
                return pe.matmul(bank_, whi, mlo, start=False, stop=stop)

            pe.wait_ge(ident_ok, 2)
            for g in range(NG):
                pe.wait_ge(x_in[g], 16)
                reach(pe, xt_done, g - 1)
                for j in range(GB):
                    mm = pe.transpose(psX[g % 2][:, j * P:(j + 1) * P], xtok[:, g * GB + j, :], ident[:, :])
                mm.then_inc(xt_ready, 1)

            def slot(T, half, c, wpar, col, dpar=None, gu=True):
                if gu:
                    for bank_, q, free, done in ((psG, 0, silu_done, g_ready), (psU, 1, mul_done, u_ready)):
                        reach(pe, free, T - 1)
                        three(bank_[c % 2][:, :], wset(wpar, 0, q, c), wset(wpar, 1, q, c),
                              xhi[:, bass.ds(col, GT)], xlo[:, bass.ds(col, GT)], True, True).then_inc(done, 1)
                if dpar is not None:
                    pe.wait_ge(lo_done, T - 3)
                    if c == 0:
                        reach(pe, y_added, T - 8)
                    three(psY[1 - half][:, :], wset(dpar, 0, 2, c), wset(dpar, 1, 2, c),
                          ring(1 - half, c, 0), ring(1 - half, c, 1), c == 0, c == FC - 1).then_inc(d_done, 1)

            def pair(T0, col, wpar, dpar0):
                for half in range(2):
                    for c in range(FC):
                        slot(T0 + (4 * half + c), half, c, wpar, col + half * GT, wpar if half else dpar0)

            pe.wait_ge(wlo_done, 3)
            for half in range(2):
                pe.wait_ge(xlo_done, half + 1)
                for c in range(FC):
                    slot(4 * half + c, half, c, 0, half * GT, 0 if half else None)
            pe.wait_ge(xlo_done, NG)
            with pe.Fori(1, NPAIR) as gp:
                pair(8 * gp, gp * (2 * GT), 0, 0)

            pe.wait_ge(l1w_in, 48)
            for i in range(4):
                reach(pe, tr_done, i - 1)
                for c in range(FC):
                    mm = pe.transpose(psX[i % 2][:, c * P:(c + 1) * P], exraw[:, i, c * P:(c + 1) * P], ident[:, :])
                mm.then_inc(tr_ready, 1)
            pe.wait_ge(tr_done, 3)
            for c in range(FC):
                mm = pe.transpose(psX[0][:, c * SHARED:(c + 1) * SHARED], fc2raw[:, c * P:(c + 1) * P],
                                  ident[0:SHARED, 0:SHARED])
            mm.then_inc(tr_ready, 1)
            pe.wait_ge(tr_done, 4)
            for c in range(FC):
                mm = pe.transpose(psX[1][:, c * P:(c + 1) * P], fc1raw[:, c, :], ident[:, :])
            mm.then_inc(tr_ready, 1)
            pe.wait_ge(hot_ok, 4)
            pe.wait_ge(tr_done, 6)
            pe.matmul(psX[0][:, 0:B], table1[:, :], hot[0:E1, 0, :], start=True, stop=True).then_inc(bias_ready, 1)
            pe.matmul(psX[1][:, 0:B], table2[:, :], hot[:, 1, :], start=True, stop=True).then_inc(bias_ready, 1)

            with pe.Fori(0, NE // 2) as p:
                for k in range(2):
                    pe.wait_ge(wlo_done, 6 * p + (6 + 3 * k))
                    pair(64 * p + 32 * (k + 1), 0, 1 - k, k)
                    with pe.Fori(1, NPAIR) as gp:
                        pair(64 * p + 8 * gp + 32 * (k + 1), gp * (2 * GT), 1 - k, 1 - k)
            for c in range(FC):
                slot(TL0 + c, 0, c, 0, 0, 0, gu=False)

            def in_range(g, a, b):
                return not isinstance(g, int) or a <= g <= b

            def l1_slot(g, half, p):
                for c in range(FC):
                    if in_range(g, 0, NG - 1):
                        if c == 0:
                            pe.wait_ge(x1lo, g + 1)
                        reach(pe, gelu_done, 4 * g + (c - 1))
                        three(psG[c % 2][:, :], fc1hi[:, c * P:(c + 1) * P], fc1lo[:, c * P:(c + 1) * P],
                              xhi[:, bass.ds(g * GT, GT)], xlo[:, bass.ds(g * GT, GT)], True, True) \
                            .then_inc(fc_ready, 1)
                    if in_range(g, 1, NG):
                        if c == 0:
                            pe.wait_ge(gelu_done, 4 * g)
                            reach(pe, x2_done, 4 * g - 8)
                        pe.wait_ge(w2_ready, 4 * g + (c - 3))
                        for i in range(FC):
                            mm = pe.matmul(psY[1 - half][:, c * P:(c + 1) * P], w2[:, 1 - half, c, i, :],
                                           h1[:, 1 - half, i, c * P:(c + 1) * P], start=i == 0, stop=i == FC - 1)
                        mm.then_inc(l1_ready, 1)
                if in_range(g, 2, NG + 1):
                    pe.wait_ge(x2_done, 4 * g - 4)
                    pe.wait_ge(cat_in[half], 64 * p)
                    for j in range(GB):
                        mm = pe.matmul(psX[half][:, j * P:(j + 1) * P], wcat[:, half, j, :],
                                       xT[:, bass.ds(g * GT + (j * P - 2 * GT), P)], start=True, stop=True)
                    mm.then_inc(l2_ready, 1)

            pe.wait_ge(fc1lo_ok, 1)
            pe.wait_ge(bias_ok, 2)
            pe.wait_ge(silu_done, TL0)
            pe.wait_ge(fc2_ok, 2 * GB - 1)
            for g in range(2):
                if g == 1:
                    pe.wait_ge(y_added, TL0)
                l1_slot(g, g, 0)
            with pe.Fori(1, NPAIR) as p:
                for half in range(2):
                    l1_slot(2 * p + half, half, p)
            for half in range(2):
                l1_slot(NG + half, half, NPAIR)

            def expert_of(g, j):
                return pe.value_load(idxs[0:1, 2, bass.ds(4 * g + j, 1)], min_val=0, max_val=E3 - 1)

            def expert_in(g, half, j):
                n = expert_of(g, j)
                mhi, mlo = xs_hi[:, half, j * P:(j + 1) * P], xs_lo[:, half, j * P:(j + 1) * P]
                for bank_, w, free, done in ((psG, 0, gelu3, g3), (psU, 1, mul3, u3)):
                    reach(pe, free, 8 * g + 2 * j)
                    whi = rbuf[:, bass.ds(n * EXP_STEP + (EXP_AT + w * 2 * F), F)]
                    wlo = rbuf[:, bass.ds(n * EXP_STEP + (EXP_AT + w * 2 * F + F), F)]
                    three(bank_[1][:, :], mhi, mlo, whi, wlo, True, True).then_inc(done, 1)

            def shared_in(g, half, c):
                for bank_, q, free, done in ((psG, 0, gelu3, g3), (psU, 1, mul3, u3)):
                    reach(pe, free, 8 * g + (2 * c - 1))
                    three(bank_[0][:, :], wset(1, 0, q, c), wset(1, 1, q, c), xs_hi[:, half, :], xs_lo[:, half, :],
                          True, True).then_inc(done, 1)

            def shared_down(g, c):
                pe.wait_ge(slo, 4 * g + (c + 1))
                if c == 0:
                    reach(pe, s_out, g)
                mm = three(psY[0][:, :], wset(1, 0, 2, c), wset(1, 1, 2, c), shid(c, 0), shid(c, 1),
                           c == 0, c == FC - 1)
                mm.then_inc(d_done, 1)

            def turn(g, j):
                pe.wait_ge(mul3, 8 * g + (2 * j + 2))
                reach(pe, t_out, 4 * g + j)
                for c in range(FC):
                    mm = pe.transpose(psX[0][:, c * P:(c + 1) * P], hid[:, (2 * j + 1) % 4, c * P:(c + 1) * P],
                                      ident[:, :])
                mm.then_inc(t_ready, 1)

            def expert_down(g, j):
                n = expert_of(g, j)
                pe.wait_ge(t_out, 4 * g + (j + 1))
                if j == 0:
                    reach(pe, e_out, g)
                for c in range(FC):
                    mm = pe.matmul(psY[1][:, j * P:(j + 1) * P], hT[:, j % 2, c * P:(c + 1) * P],
                                   woe[:, bass.ds(n, 1), c, :].rearrange("p a n -> p (a n)"),
                                   start=c == 0, stop=c == FC - 1)
                mm.then_inc(e_done, 1)

            def mix(p, half, k):
                if (half, k) == (0, 6):
                    pe.wait_ge(e0_in, 16 * p + 16)
                    reach(pe, o_done, 8 * p)
                    pe.matmul(psX[1][:, 0:2 * GB], e0r[:, :], ident[0:2 * GB, 0:2 * GB], start=True,
                              stop=True).then_inc(gate_pe, 1)
                if (half, k) == (0, 7):
                    pe.wait_ge(gate_dve, 9 * p + 2)
                    pe.matmul(psX[1][:, 8:8 + 2 * GB], g0s[:, 0, :], gE[:, :], start=True, stop=False)
                    pe.matmul(psX[1][:, 8:8 + 2 * GB], g0s[:, 1, :], gS[:, :], start=False, stop=True) \
                        .then_inc(gate_pe, 1)
                if (half, k) == (1, 0):
                    pe.wait_ge(gate_dve, 9 * p + 3)
                    for a in range(2):
                        mm = pe.matmul(psX[1][:, 16 + a * 2 * GB:16 + (a + 1) * 2 * GB], g1b[:, a, :], ghid[:, :],
                                       start=True, stop=True)
                    mm.then_inc(gate_pe, 1)
                for a in range(2):
                    if (half, k) == (1, 2 + 2 * a):
                        pe.wait_ge(z_done, 8 * p + (4 * a + 4))
                        reach(pe, o_done, 8 * p + 4 * a)
                        for j in range(GB):
                            mm = pe.transpose(psX[1][:, j * P:(j + 1) * P], z[:, a, j, :], ident[:, :])
                        mm.then_inc(z_ready, 1)

            def l3_slot(g, half, p=None, first=False, stream=True):
                for k in range(8):
                    if stream:
                        if k == 0:
                            pe.wait_ge(xslo, g + 1)
                        (expert_in if k % 2 else shared_in)(g, half, k // 2)
                    late = not first or k >= 2
                    if k % 2 == 0 and late and (stream or k == 0):
                        shared_down(*((g, k // 2 - 1) if k else (g - 1, FC - 1)))
                    if k % 2 == 1:
                        if (not first or k >= 5) and (stream or k <= 3):
                            expert_down(*((g, k // 2 - 2) if k >= 5 else (g - 1, k // 2 + 2)))
                        if (not first or k >= 3) and (stream or k <= 1):
                            turn(*((g, k // 2 - 1) if k >= 3 else (g - 1, FC - 1)))
                    if p is not None:
                        mix(p, half, k)

            pe.wait_ge(plo_done, 2 * E3)
            pe.wait_ge(wo_in, 16 * E3)
            pe.wait_ge(x3_done, B)
            pe.wait_ge(gelu_done, TILES)
            pe.wait_ge(g1b_ok, 2)
            l3_slot(0, 0, first=True)
            l3_slot(1, 1)
            with pe.Fori(1, NPAIR - 1) as p:
                for half in range(2):
                    l3_slot(2 * p + half, half, p - 1)
            for half in range(2):
                l3_slot(NG - 2 + half, half, NPAIR - 2)
            l3_slot(NG, 0, stream=False)
            for half in range(2):
                for k in range(8):
                    mix(NPAIR - 1, half, k)


_INS = ['x', 'fside_Bx8_0', 'condB_sharedgateprob', 'itok_B_0_15', 'itok_B_0_63', 'itok_B_0_2',
        'L0_cond_Wg', 'L0_cond_Wu', 'L0_cond_Wd', 'L0_cond_Sg', 'L0_cond_Su', 'L0_cond_Sd',
        'L1_cond_fc1_w', 'L1_cond_fc1_b', 'L1_cond_fc2_w', 'L1_cond_fc2_b', 'L1_cond_experts_w', 'L1_cond_experts_b',
        'L2_cond_W', 'L2_cond_b', 'L3_cond_Wi0', 'L3_cond_Wi1', 'L3_cond_Wo',
        'L3_cond_sWi0', 'L3_cond_sWi1', 'L3_cond_sWo', 'L3_cond_g0', 'L3_cond_g1']


def kernel(**inputs):
    import numpy as np
    import concourse.bacc as bacc
    from concourse import mybir as mb
    from concourse.bass_utils import run_bass_kernel_spmd

    nc = bacc.Bacc("TRN2", target_bir_lowering=False, num_devices=1)
    arrays, args = {}, []
    for name in _INS:
        a = np.ascontiguousarray(inputs[name])
        arrays[f"in_{name}"] = a
        args.append(nc.dram_tensor(f"in_{name}", a.shape, mb.dt.from_np(a.dtype), kind="ExternalInput").ap())
    result = nc.dram_tensor("out_x", (B, P, P), mb.dt.float32, kind="ExternalOutput").ap()
    build_kernel(nc, *args, result)
    r = run_bass_kernel_spmd(nc, [arrays], core_ids=[0])
    return r.results[0]["out_x"]
```

```python
from contextlib import ExitStack

import concourse.bass as bass
from concourse import mybir

F32 = mybir.dt.float32
F32R = mybir.dt.float32r
I32 = mybir.dt.int32
ALU = mybir.AluOpType
ACT = mybir.ActivationFunctionType

P = 128
B = 32
GB = 4
GT = GB * P
NG = B // GB
NPAIR = NG // 2
FC = 4
F = FC * P
NE = 8
ROUNDS = NE + 1
E1 = 16
PART = 32
SHARED = P - PART
E2 = 64
E3 = 5
WSET = 3 * F
TILES = NG * FC
X_TILE = [3 * g for g in range(NG - 1)]
L1W_TILE = [19 + 2 * i for i in range(6)]

SET_AT = [2 * WSET, 0]
RING_AT = 4 * WSET
EXP_AT = 2 * WSET
EXP_STEP = 4 * F
RBUF = RING_AT + 2 * FC * 2 * GT
LAST_RING = (NPAIR - 1) % 2 * 2
GATE_STEPS = 12


def reach(eng, sem, value):
    if isinstance(value, int) and value <= 0:
        return
    eng.wait_ge(sem, value)


def build_kernel(nc, x, fside, sgate, idx1, idx2, idx3, Wg, Wu, Wd, Sg, Su, Sd,
                 fc1_w, fc1_b, fc2_w, fc2_b, ex_w, ex_b, W2, b2,
                 Wi0, Wi1, Wo, sWi0, sWi1, sWo, g0, g1, out):
    with ExitStack() as ctx:
        def sb(name, shape, dt=F32):
            return ctx.enter_context(nc.sbuf_tensor(name, shape, dt))

        def bank(name):
            return ctx.enter_context(nc.psum_tensor(name, [P, GT], F32))

        def sem(name):
            return ctx.enter_context(nc.semaphore(name))

        psG = [bank("psG0"), bank("psG1")]
        psU = [bank("psU0"), bank("psU1")]
        psY = [bank("psY0"), bank("psY1")]
        psX = [bank("psX0"), bank("psX1")]

        xT = sb("xT", [P, B * P])
        xhi = sb("xhi", [P, B * P], F32R)
        xlo = sb("xlo", [P, B * P], F32R)
        rbuf = sb("rbuf", [P, RBUF], F32R)
        raw = sb("raw", [P, 2, WSET])
        act = sb("act", [P, 2, GT])
        hid = sb("hid", [P, 4, GT])
        h1 = sb("h1", [P, 2, FC, GT])
        ident = sb("ident", [P, P])
        gates = sb("gates", [P, ROUNDS * B])
        fs = sb("fs", [P, B * NE])
        omg = sb("omg", [P, B])
        fc1hi = sb("fc1hi", [P, F], F32R)
        fc1lo = sb("fc1lo", [P, F], F32R)
        fc1T = sb("fc1T", [P, F])
        fc1b = sb("fc1b", [P, FC])
        exT = sb("exT", [P, E1, FC, PART])
        w2 = sb("w2", [P, 2, GB, FC, P])
        bias1 = sb("bias1", [P, B])
        bias2 = sb("bias2", [P, B])
        idxs = sb("idxs", [1, 3, B], I32)
        hot = sb("hot", [E2, 2, B])
        wcat = sb("wcat", [P, 2, GB, P])
        woe = sb("woe", [P, E3, FC, P])
        g1b = sb("g1b", [P, 2, P])
        g0s = sb("g0s", [P, 2, P])
        xs_hi = sb("xs_hi", [P, 2, GT], F32R)
        xs_lo = sb("xs_lo", [P, 2, GT], F32R)
        idxb = sb("idxb", [E2, 2, B], I32)
        idxf = sb("idxf", [E2, 2, B])
        row_id = sb("row_id", [E2, 1], I32)
        row_f = sb("row_f", [E2, 1])
        table1 = sb("table1", [E1, P])
        table2 = sb("table2", [E2, P])
        e0r = sb("e0r", [2 * GB, P])
        g1s = sb("g1s", [P, 2])
        gE = sb("gE", [P, 2 * GB])
        gS = sb("gS", [P, 2 * GB])
        ghid = sb("ghid", [P, 2 * GB])
        glog = sb("glog", [P, 2, 2 * GB])
        gmax = sb("gmax", [P, 2 * GB])
        gdiff = sb("gdiff", [P, 2, 2 * GB])
        gtanh = sb("gtanh", [P, 2, 2 * GB])
        gnum = sb("gnum", [P, 2, 2 * GB])
        gden = sb("gden", [P, 2, 2 * GB])
        gexp = sb("gexp", [P, 2, 2 * GB])
        gsum = sb("gsum", [P, 2 * GB])
        grec = sb("grec", [P, 2 * GB])
        gw = sb("gw", [P, 2, 2 * GB])

        h1f = h1[:, :, :, :].rearrange("p a c n -> p (a c n)")
        xtok = h1f.rearrange("p (b d) -> p b d", b=B)
        hT = h1f[:, 0:2 * F].rearrange("p (a n) -> p a n", a=2)
        esb = h1f[:, 2 * F:6 * F].rearrange("p (a j n) -> p a j n", a=2 * 2, j=GB)
        osb = h1f[:, 6 * F:8 * F].rearrange("p (a j n) -> p a j n", a=2, j=GB)
        w2f = w2[:, :, :, :, :].rearrange("p a j c n -> p (a j c n)")
        z = w2f[:, 0:2 * GT].rearrange("p (a j n) -> p a j n", a=2, j=GB)
        part = z
        last_e = w2f[:, 6 * GT:8 * GT].rearrange("p (a j n) -> p a j n", a=2, j=GB)
        ssb = w2f[:, 2 * GT:6 * GT].rearrange("p (a j n) -> p a j n", a=2 * 2, j=GB)
        exraw = woe[:, :, :, :].rearrange("p e c n -> p (e c n)")[:, 0:4 * F].rearrange("p (r f) -> p r f", r=4)
        fc2raw = wcat[0:SHARED, 0, :, :].rearrange("p j n -> p (j n)")
        fc1raw = wcat[:, 1, :, :]

        def wset(par, lo, q, c):
            at = SET_AT[par] + lo * WSET + q * F + c * P
            return rbuf[:, at:at + P]

        def shid(c, lo):
            return (xlo if lo else xhi)[:, c * GT:(c + 1) * GT]

        def ring(half, c, lo):
            at = RING_AT + (half * FC + c) * 2 * GT + lo * GT
            return rbuf[:, at:at + GT]

        x_in = [sem(f"x_in{g}") for g in range(NG)]
        small_in, idx_in, l1w_in, g_in = sem("small_in"), sem("idx_in"), sem("l1w_in"), sem("g_in")
        first_in = [sem("first_in0"), sem("first_in1"), sem("first_in2")]
        raw_in = [sem("raw_in0"), sem("raw_in1")]
        cat_in = [sem("cat_in0"), sem("cat_in1")]
        wo_in, e0_in, out_sem = sem("wo_in"), sem("e0_in"), [sem("out_sem0"), sem("out_sem1")]
        ident_ok, hot_ok = sem("ident_ok"), sem("hot_ok")
        xt_ready, xt_done, xhi_done, xlo_done = sem("xt_ready"), sem("xt_done"), sem("xhi_done"), sem("xlo_done")
        sg_hi, gates_ok, g1b_ok = sem("sg_hi"), sem("gates_ok"), sem("g1b_ok")
        tr_ready, tr_done, fc1hi_ok, fc1lo_ok, fc2_ok = (sem("tr_ready"), sem("tr_done"), sem("fc1hi_ok"),
                                                         sem("fc1lo_ok"), sem("fc2_ok"))
        bias_ready, bias_ok = sem("bias_ready"), sem("bias_ok")
        whi_done, wlo_done = sem("whi_done"), sem("wlo_done")
        g_ready, u_ready, d_done = sem("g_ready"), sem("u_ready"), sem("d_done")
        silu_done, mul_done, hi_done, lo_done, y_added = (sem("silu_done"), sem("mul_done"), sem("hi_done"),
                                                          sem("lo_done"), sem("y_added"))
        fc_ready, gelu_done, l1_ready, l2_ready = sem("fc_ready"), sem("gelu_done"), sem("l1_ready"), sem("l2_ready")
        x1hi, x1lo, x2_done, x3_done, w2_ready = (sem("x1hi"), sem("x1lo"), sem("x2_done"), sem("x3_done"),
                                                  sem("w2_ready"))
        p_in, last_in = [sem("p_in0"), sem("p_in1")], sem("last_in")
        phi_done, plo_done = sem("phi_done"), sem("plo_done")
        xshi, xslo = sem("xshi"), sem("xslo")
        g3, u3, gelu3, mul3 = sem("g3"), sem("u3"), sem("gelu3"), sem("mul3")
        shi, slo, s_out = sem("shi"), sem("slo"), sem("s_out")
        t_ready, t_out, e_done, e_out = sem("t_ready"), sem("t_out"), sem("e_done"), sem("e_out")
        gate_pe, gate_dve, gate_half, gate_act, last_scaled, last_turned, z_done, z_ready, o_done = (sem("gate_pe"), sem("gate_dve"), sem("gate_half"), sem("gate_act"), sem("last_scaled"), sem("last_turned"),
                                                                sem("z_done"), sem("z_ready"), sem("o_done"))

        TL0 = ROUNDS * TILES

        block = ctx.enter_context(nc.Block())

        @block.sync
        def _(sp):
            def load_raw(par, gate, up, down, free):
                if free is not None:
                    sp.wait_ge(wlo_done, free)
                for q, w in ((0, gate), (1, up)):
                    sp.dma_start(raw[:, par, q * F:(q + 1) * F], w).then_inc(raw_in[par], 16)
                sp.dma_start(raw[:, par, 2 * F:3 * F].rearrange("p (c d) -> p c d", c=FC),
                             down.rearrange("(c p) d -> p c d", p=P)).then_inc(raw_in[par], 16)

            def load_x(g):
                sp.dma_start(xtok[:, g * GB:(g + 1) * GB, :],
                             x[g * GB:(g + 1) * GB].rearrange("b n d -> n b d")).then_inc(x_in[g], 16)

            load_x(0)
            sp.dma_start(raw[:, 0, 0:F], Sg).then_inc(first_in[0], 16)
            sp.dma_start(raw[:, 0, F:2 * F], Su).then_inc(first_in[1], 16)
            load_x(1)
            sp.dma_start(raw[:, 0, 2 * F:3 * F].rearrange("p (c d) -> p c d", c=FC),
                         Sd.rearrange("(c p) d -> p c d", p=P)).then_inc(first_in[2], 16)
            load_x(2)
            sp.dma_start(gates[:, 0:B], sgate.partition_broadcast(P)).then_inc(small_in, 16)
            sp.dma_start(fs[:, :], fside.rearrange("b e -> (b e)").partition_broadcast(P)).then_inc(small_in, 16)
            for g in range(3, NG):
                load_x(g)
            load_raw(1, Wg[0], Wu[0], Wd[0], None)
            sp.dma_start(exraw, ex_w.rearrange("e p f -> (e p) f").rearrange("(r q) f -> q r f", q=P)) \
                .then_inc(l1w_in, 16)
            sp.dma_start(fc2raw, fc2_w).then_inc(l1w_in, 16)
            sp.dma_start(fc1raw, fc1_w.rearrange("(c q) d -> q c d", q=P)).then_inc(l1w_in, 16)
            sp.dma_start(idxb[:, 0, :], idx1.partition_broadcast(E2)).then_inc(g_in, 16)
            sp.dma_start(idxb[:, 1, :], idx2.partition_broadcast(E2)).then_inc(g_in, 16)
            sp.dma_start(table1[:, SHARED:P], ex_b).then_inc(g_in, 16)
            sp.dma_start(table1[:, 0:SHARED], fc2_b.partition_broadcast(E1)).then_inc(g_in, 16)
            sp.dma_start(table2[:, :], b2).then_inc(g_in, 16)
            with nc.allow_non_contiguous_dma(reason="128 x 4 and 128 x 2 numbers"):
                sp.dma_start(fc1b[:, :], fc1_b.rearrange("(c p) -> p c", p=P)).then_inc(g_in, 16)
                sp.dma_start(g1s[:, :], g1).then_inc(g_in, 16)
            sp.dma_start(g0s[:, :, :], g0.rearrange("(a p) d -> p a d", p=P)).then_inc(g_in, 16)
            sp.dma_start(idxs[0:1, 0, :], idx1.rearrange("(a b) -> a b", a=1)).then_inc(idx_in, 16)
            sp.dma_start(idxs[0:1, 1, :], idx2.rearrange("(a b) -> a b", a=1)).then_inc(idx_in, 16)
            sp.dma_start(idxs[0:1, 2, :], idx3.rearrange("(a b) -> a b", a=1)).then_inc(idx_in, 16)
            with sp.Fori(1, NPAIR) as p:
                load_raw(0, Wg[bass.ds(2 * p - 1, 1)].rearrange("a d f -> (a d) f"),
                         Wu[bass.ds(2 * p - 1, 1)].rearrange("a d f -> (a d) f"),
                         Wd[bass.ds(2 * p - 1, 1)].rearrange("a d f -> (a d) f"), 6 * p - 3)
                load_raw(1, Wg[bass.ds(2 * p, 1)].rearrange("a d f -> (a d) f"),
                         Wu[bass.ds(2 * p, 1)].rearrange("a d f -> (a d) f"),
                         Wd[bass.ds(2 * p, 1)].rearrange("a d f -> (a d) f"), 6 * p)
            load_raw(0, Wg[NE - 1], Wu[NE - 1], Wd[NE - 1], 3 * (ROUNDS - 2))
            load_raw(1, sWi0, sWi1, sWo, 3 * (ROUNDS - 1))
            sp.wait_ge(tr_done, 6)
            for e in range(E3):
                sp.dma_start(woe[:, e, :, :], Wo[e].rearrange("(c p) d -> p c d", p=P)).then_inc(wo_in, 16)

            def load_cat(b, half, j):
                n = sp.value_load(idxs[0:1, 1, b], min_val=0, max_val=E2 - 1)
                sp.dma_start(wcat[:, half, j, :], W2[bass.ds(n, 1)].rearrange("a d h -> (a d) h")) \
                    .then_inc(cat_in[half], 16)

            def load_piece(half, e, free):
                if free is not None:
                    sp.wait_ge(plo_done, free)
                w = (Wi0, Wi1)[half]
                src = w[e] if isinstance(e, int) else w[bass.ds(e, 1)].rearrange("a d f -> (a d) f")
                sp.dma_start(raw[:, half, 0:F], src).then_inc(p_in[half], 16)

            sp.wait_ge(idx_in, 48)
            for half in range(2):
                for j in range(GB):
                    load_cat(bass.ds(half * GB + j, 1), half, j)
            sp.wait_ge(wlo_done, 3 * (ROUNDS + 1))
            for half in range(2):
                load_piece(half, 0, None)
            for half in range(2):
                sp.dma_start(raw[:, half, F:2 * F], (Wi0, Wi1)[half][E3 - 1]).then_inc(last_in, 16)
            def load_cats(p, half):
                sp.wait_ge(l2_ready, 2 * p + half - 1)
                for j in range(GB):
                    load_cat(bass.ds(8 * p + (half * GB + j), 1), half, j)

            for half in range(2):
                load_piece(half, 1, half + 3)
            with sp.Fori(1, NPAIR - 1) as p:
                for half in range(2):
                    load_cats(p, half)
                    load_piece(half, p + 1, 2 * p + half + 3)
            for half in range(2):
                load_cats(NPAIR - 1, half)

            def store(p, half):
                last = isinstance(p, int)
                sp.wait_ge(o_done, 2 * GB * p + (half + 1 if last else GB * (half + 1)))
                b0 = 8 * p + half * GB
                dst = out[b0:b0 + GB] if last else out[bass.ds(b0, GB)]
                sp.dma_start(dst.rearrange("b n d -> n b d"), osb[:, half, :, :]).then_inc(out_sem[half], 16)

            def finish_pair(p):
                sp.wait_ge(e_out, 2 * p + 2)
                sp.dma_start(e0r[:, :], esb[0:1, bass.ds(p % 2 * 2, 2), :, :].rearrange("o a j n -> o (a j) n")) \
                    .then_inc(e0_in, 16)
                for half in range(2):
                    store(p, half)

            with sp.Fori(0, NPAIR - 1) as p:
                finish_pair(p)
            for half in range(2):
                store(NPAIR - 1, half)
            for half in range(2):
                sp.wait_ge(out_sem[half], 16 * NPAIR)

        @block.gpsimd
        def _(pool):
            pool.memset(ident[:, :], 0.0).then_inc(ident_ok, 1)
            pool.wait_ge(ident_ok, 1)
            pool.affine_select(out=ident[:, :], in_=ident[:, :], compare_op=ALU.not_equal, fill=1.0, base=0,
                               pattern=[[-1, P]], channel_multiplier=1).then_inc(ident_ok, 1)
            pool.iota(row_id[:, :], pattern=[[0, 1]], base=0, channel_multiplier=1).then_inc(hot_ok, 1)
            pool.wait_ge(tr_done, 5)
            for s in range(1, 2 * GB):
                pool.tensor_copy(w2[:, s // GB, s % GB, :, 0:SHARED], w2[:, 0, 0, :, 0:SHARED]).then_inc(fc2_ok, 1)
            pool.wait_ge(tr_done, 6)
            pool.wait_ge(idx_in, 48)

            def expert_columns(b, half, j, free):
                n = pool.value_load(idxs[0:1, 0, b], min_val=0, max_val=E1 - 1)
                if free is not None:
                    pool.wait_ge(l1_ready, free)
                pool.tensor_copy(w2[:, half, j, :, SHARED:P],
                                 exT[:, bass.ds(n, 1), :, :].rearrange("p a c n -> p (a c) n")).then_inc(w2_ready, 1)

            for s in range(2 * GB):
                expert_columns(bass.ds(s, 1), s // GB, s % GB, None)
            with pool.Fori(1, NPAIR) as p:
                for s in range(2 * GB):
                    expert_columns(bass.ds(8 * p + s, 1), s // GB, s % GB, 8 * p + (s - 7))

        @block.scalar
        def _(sc):
            def x_hi(g):
                sc.wait_ge(xt_done, g + 1)
                sc.activation(xhi[:, g * GT:(g + 1) * GT], xT[:, g * GT:(g + 1) * GT], ACT.Copy).then_inc(xhi_done, 1)

            def first_hi(q):
                sc.wait_ge(first_in[q], 16)
                sc.activation(rbuf[:, SET_AT[0] + q * F:SET_AT[0] + (q + 1) * F], raw[:, 0, q * F:(q + 1) * F],
                              ACT.Copy).then_inc(whi_done, 1)

            def slot(p, s, hi=True, gu=True):
                T, c = 64 * p + s, s % FC
                if gu:
                    sc.wait_ge(g_ready, T + 1)
                    reach(sc, mul_done, T - 1)
                    sc.activation(act[:, c % 2, :], psG[c % 2][:, :], ACT.Silu).then_inc(silu_done, 1)
                if hi:
                    sc.wait_ge(mul_done, T)
                    reach(sc, d_done, T - 8)
                    k = (s - 1) % FC
                    sc.activation(ring((s - 1) // FC % 2, k, 0), hid[:, k, :], ACT.Copy).then_inc(hi_done, 1)

            def split_third(p, r, third):
                par = (r + 1) % 2
                sc.wait_ge(raw_in[par], 48 * p + 48 * ((r + 1 + par) // 2))
                reach(sc, d_done, 64 * p + TILES * r)
                at = SET_AT[par] + third * F
                sc.activation(rbuf[:, at:at + F], raw[:, par, third * F:(third + 1) * F], ACT.Copy) \
                    .then_inc(whi_done, 1)

            def round_(p, r):
                for t in range(TILES):
                    s = TILES * r + t
                    slot(p, s, hi=s > 0)
                    if r == 0 and t - 1 in X_TILE:
                        x_hi(X_TILE.index(t - 1) + 1)
                    if t % 8 == 1 and t > 8:
                        split_third(p, r, t // 8 - 1)

            sc.wait_ge(ident_ok, 2)
            sc.activation(act[0:1, 0, 0:1], ident[0:1, 0:1], ACT.Silu)
            x_hi(0)
            for q in (1, 2):
                first_hi(q)
            round_(0, 0)
            sc.wait_ge(tr_done, 6)
            sc.activation(fc1hi[:, :], fc1T[:, :], ACT.Copy).then_inc(fc1hi_ok, 1)
            with sc.Fori(0, NE // 2) as p:
                for r in (1, 2):
                    round_(p, r)

            def split_x1(g):
                sc.wait_ge(y_added, 4 * g + (TL0 - TILES + 4))
                sc.wait_ge(u_ready, 4 * g + (TL0 - TILES + 4))
                sc.activation(xhi[:, bass.ds(g * GT, GT)], xT[:, bass.ds(g * GT, GT)], ACT.Copy).then_inc(x1hi, 1)

            def l1_slot(g, half, e, last_expert=False):
                for c in range(FC):
                    sc.wait_ge(fc_ready, 4 * g + (c + 1))
                    if c == 0:
                        reach(sc, l1_ready, 4 * g - 4)
                    sc.activation(h1[:, half, c, :], psG[c % 2][:, :], ACT.Gelu, bias=fc1b[:, c:c + 1]) \
                        .then_inc(gelu_done, 1)
                    if c == (3 if isinstance(g, int) and g == 0 else 1):
                        sc.wait_ge(p_in[half], 16 * e + 16)
                        sc.wait_ge(d_done, TL0)
                        at = EXP_AT + half * 2 * F
                        sc.activation(rbuf[:, bass.ds(e * EXP_STEP + at, F)], raw[:, half, 0:F], ACT.Copy) \
                            .then_inc(phi_done, 1)
                    if c == 3 and (not isinstance(g, int) or g + 2 < NG):
                        split_x1(g + 2)
                if last_expert:
                    for w in range(2):
                        sc.wait_ge(last_in, 32)
                        at = EXP_AT + (E3 - 1) * EXP_STEP + w * 2 * F
                        sc.activation(rbuf[:, at:at + F], raw[:, w, F:2 * F], ACT.Copy).then_inc(phi_done, 1)

            sc.wait_ge(g_in, 16 * 8)
            split_x1(0)
            slot(0, TL0, gu=False)
            split_x1(1)
            for half in range(2):
                l1_slot(half, half, 0, last_expert=half == 1)
            with sc.Fori(1, NPAIR - 1) as p:
                for half in range(2):
                    l1_slot(2 * p + half, half, p)
            def split_x3(g, half):
                sc.wait_ge(x3_done, 4 * g + 4)
                reach(sc, u3, 8 * g - 8)
                sc.activation(xs_hi[:, half, :], xT[:, bass.ds(g * GT, GT)], ACT.Copy).then_inc(xshi, 1)

            l1_slot(NG - 2, 0, NPAIR - 1)
            split_x3(0, 0)
            l1_slot(NG - 1, 1, NPAIR - 1)

            def l3_slot(g, half, first=False, last=False, stream=True, mix=None):
                for k in range(8):
                    K = 8 * g + k
                    if stream:
                        sc.wait_ge(g3, K + 1)
                        reach(sc, mul3, K - 1)
                        sc.activation(act[:, k % 2, :], psG[k % 2][:, :], ACT.Gelu_apprx_tanh).then_inc(gelu3, 1)
                        if k % 2 == 1:
                            q = 4 * g + (k - 1) // 2
                            sc.wait_ge(mul3, K)
                            reach(sc, d_done, q - 3 + TL0)
                            sc.activation(shid((k - 1) // 2, 0), hid[:, (k - 1) % 4, :], ACT.Copy).then_inc(shi, 1)
                    if k % 2 == 0 and (not first or k >= 4) and (stream or k < 4):
                        r = 4 * g + (k // 2 - 2)
                        sc.wait_ge(t_ready, r + 1)
                        reach(sc, e_done, r - 1)
                        sc.activation(hT[:, (k // 2) % 2, :], psX[0][:, :], ACT.Copy).then_inc(t_out, 1)
                    if k == 1 and mix is not None:
                        gate_tanh(mix)
                    if k == 1 and not first:
                        sc.wait_ge(d_done, 4 * g + TL0)
                        sc.activation(ssb[:, bass.ds((g + 3) % 4, 1), :, :].rearrange("p a j n -> p (a j n)"),
                                      psY[0][:, :], ACT.Copy) \
                            .then_inc(s_out, 1)
                    if k == 4 and not first:
                        sc.wait_ge(e_done, 4 * g)
                        sc.activation(esb[:, bass.ds((g + 3) % 4, 1), :, :].rearrange("p a j n -> p (a j n)"),
                                      psY[1][:, :], ACT.Copy) \
                            .then_inc(e_out, 1)
                    if k == 2 and not last and stream:
                        split_x3(g + 1, 1 - half)

            def gate_tanh(p):
                sc.wait_ge(gate_dve, GATE_STEPS * p + 6)
                sc.activation(gtanh[:, :, :], gdiff[:, :, :], ACT.Tanh, scale=0.5).then_inc(gate_act, 1)

            l3_slot(0, 0, first=True)
            l3_slot(1, 1)
            with sc.Fori(1, NPAIR - 1) as p:
                l3_slot(2 * p, 0)
                l3_slot(2 * p + 1, 1, mix=p - 1)
            l3_slot(NG - 2, 0)
            l3_slot(NG - 1, 1, last=True, mix=NPAIR - 2)
            l3_slot(NG, 0, stream=False)
            gate_tanh(NPAIR - 1)
            sc.wait_ge(gate_dve, GATE_STEPS * NPAIR)
            for n in range(2 * GB):
                sc.activation(last_e[:, n // GB, n % GB, :], esb[:, LAST_RING + n // GB, n % GB, :], ACT.Identity,
                              scale=gw[:, 0, n:n + 1]).then_inc(last_scaled, 1)

        @block.vector
        def _(ve):
            def split_lo(dst, value, hi, done):
                ve.tensor_tensor(dst, value, hi.bitcast(F32), ALU.subtract).then_inc(done, 1)

            def x_out(g):
                ve.wait_ge(xt_ready, g + 1)
                ve.tensor_copy(xT[:, g * GT:(g + 1) * GT], psX[g % 2][:, :]).then_inc(xt_done, 1)

            def x_lo(g):
                ve.wait_ge(xhi_done, g + 1)
                ve.wait_ge(xt_done, g + 1)
                split_lo(xlo[:, g * GT:(g + 1) * GT], xT[:, g * GT:(g + 1) * GT], xhi[:, g * GT:(g + 1) * GT],
                         xlo_done)

            def first_lo(q):
                ve.wait_ge(*((whi_done, q) if q else (sg_hi, 1)))
                ve.wait_ge(first_in[q], 16)
                split_lo(rbuf[:, SET_AT[0] + WSET + q * F:SET_AT[0] + WSET + (q + 1) * F],
                         raw[:, 0, q * F:(q + 1) * F], rbuf[:, SET_AT[0] + q * F:SET_AT[0] + (q + 1) * F], wlo_done)

            def weigh():
                ve.wait_ge(small_in, 32)
                ve.tensor_scalar(omg[:, :], gates[:, 0:B], -1.0, 1.0, ALU.mult, ALU.add).then_inc(gates_ok, 1)
                ve.wait_ge(gates_ok, 1)
                ve.tensor_tensor(gates[:, B:ROUNDS * B].rearrange("p (e b) -> p e b", e=NE),
                                 fs[:, :].rearrange("p (b e) -> p e b", e=NE),
                                 omg[:, :].unsqueeze(1).to_broadcast([P, NE, B]), ALU.mult).then_inc(gates_ok, 1)

            def add_piece(p, s):
                T, c = 64 * p + s, s % FC
                ve.wait_ge(d_done, T - (8 - FC) - c)
                xb = xT[:, (s - 8) % B * P:((s - 8) % B + 1) * P]
                ve.scalar_tensor_tensor(out=xb, in0=psY[s // FC % 2][:, c * P:(c + 1) * P],
                                        scalar=gates[:, bass.ds(T - 8, 1)], in1=xb,
                                        op0=ALU.mult, op1=ALU.add).then_inc(y_added, 1)

            def lo_part(p, s):
                T, k, half = 64 * p + s, (s - 1) % FC, (s - 1) // FC % 2
                ve.wait_ge(hi_done, T)
                ve.wait_ge(mul_done, T)
                reach(ve, d_done, T - 8)
                split_lo(ring(half, k, 1), hid[:, k, :], ring(half, k, 0), lo_done)

            def slot(p, s, head=False):
                T, c = 64 * p + s, s % FC
                ve.wait_ge(silu_done, T + 1)
                ve.wait_ge(u_ready, T + 1)
                reach(ve, lo_done, T - 3)
                ve.tensor_tensor(hid[:, c, :], act[:, c % 2, :], psU[c % 2][:, :], ALU.mult).then_inc(mul_done, 1)
                if not head or s >= 8:
                    add_piece(p, s)
                if not head or s > 0:
                    lo_part(p, s)

            def third_lo(p, r, third):
                par = (r + 1) % 2
                ve.wait_ge(whi_done, 6 * p + (3 * (r + 1) + third))
                at = SET_AT[par] + third * F
                split_lo(rbuf[:, at + WSET:at + WSET + F], raw[:, par, third * F:(third + 1) * F],
                         rbuf[:, at:at + F], wlo_done)

            def l1_weights(i):
                ve.wait_ge(tr_ready, i + 1)
                if i < 4:
                    dst = exT[:, 4 * i:4 * i + 4, :, :].rearrange("p e c n -> p c e n")
                    src = psX[i % 2][:, :].rearrange("p (c e n) -> p c e n", c=FC, e=4)
                elif i == 4:
                    dst = w2[:, 0, 0, :, 0:SHARED]
                    src = psX[0][:, 0:FC * SHARED].rearrange("p (c n) -> p c n", c=FC)
                else:
                    dst, src = fc1T[:, :], psX[1][:, :]
                ve.tensor_copy(dst, src).then_inc(tr_done, 1)

            def one_hot():
                ve.wait_ge(hot_ok, 1)
                ve.wait_ge(g_in, 16 * 8)
                ve.tensor_copy(row_f[:, :], row_id[:, :]).then_inc(hot_ok, 1)
                ve.tensor_copy(idxf[:, :, :], idxb[:, :, :]).then_inc(hot_ok, 1)
                ve.wait_ge(hot_ok, 3)
                ve.tensor_scalar(hot[:, :, :], idxf[:, :, :], row_f[:, 0:1], None, ALU.is_equal).then_inc(hot_ok, 1)

            def round_(p, r):
                for t in range(TILES):
                    s = TILES * r + t
                    slot(p, s, head=r == 0)
                    if r == 0:
                        if t == 0:
                            first_lo(2)
                        if t in X_TILE:
                            x_out(X_TILE.index(t) + 1)
                        if t - 2 in X_TILE:
                            x_lo(X_TILE.index(t - 2) + 1)
                        if t == 4:
                            weigh()
                        if t == 22:
                            one_hot()
                        if t - 1 in L1W_TILE:
                            l1_weights(L1W_TILE.index(t - 1))
                    if t % 8 == 2 and t > 8:
                        third_lo(p, r, t // 8 - 1)

            x_out(0)
            ve.wait_ge(first_in[0], 16)
            ve.tensor_copy(rbuf[:, SET_AT[0]:SET_AT[0] + F], raw[:, 0, 0:F]).then_inc(sg_hi, 1)
            first_lo(0)
            x_lo(0)
            first_lo(1)
            round_(0, 0)
            ve.wait_ge(bias_ready, 2)
            ve.tensor_copy(bias1[:, :], psX[0][:, 0:B]).then_inc(bias_ok, 1)
            ve.tensor_copy(bias2[:, :], psX[1][:, 0:B]).then_inc(bias_ok, 1)
            for a in range(2):
                ve.tensor_copy(g1b[:, a, :], g1s[:, a:a + 1].to_broadcast([P, P])).then_inc(g1b_ok, 1)
            ve.wait_ge(fc1hi_ok, 1)
            split_lo(fc1lo[:, :], fc1T[:, :], fc1hi[:, :], fc1lo_ok)
            with ve.Fori(0, NE // 2) as p:
                for r in (1, 2):
                    round_(p, r)

            def x1_lo(g):
                ve.wait_ge(x1hi, g + 1)
                split_lo(xlo[:, bass.ds(g * GT, GT)], xT[:, bass.ds(g * GT, GT)], xhi[:, bass.ds(g * GT, GT)], x1lo)

            def residual(g, src, bias, done):
                for j in range(GB):
                    xb = xT[:, bass.ds(g * GT + j * P, P)]
                    ve.scalar_tensor_tensor(out=xb, in0=src[:, j * P:(j + 1) * P],
                                            scalar=bias[:, bass.ds(4 * g + j, 1)], in1=xb,
                                            op0=ALU.add, op1=ALU.add).then_inc(done, 1)

            def x3_lo(g, half):
                ve.wait_ge(xshi, g + 1)
                split_lo(xs_lo[:, half, :], xT[:, bass.ds(g * GT, GT)], xs_hi[:, half, :], xslo)

            def add_l1(g):
                ve.wait_ge(l1_ready, 4 * g + 4)
                residual(g, psY[g % 2], bias1, x2_done)

            def add_l2(g):
                ve.wait_ge(l2_ready, g + 1)
                residual(g, psX[g % 2], bias2, x3_done)

            def piece_lo(e, half, at_raw, count):
                ve.wait_ge(phi_done, count)
                at = EXP_AT + half * 2 * F
                split_lo(rbuf[:, e * EXP_STEP + (at + F):e * EXP_STEP + (at + 2 * F)], raw[:, half, at_raw:at_raw + F],
                         rbuf[:, e * EXP_STEP + at:e * EXP_STEP + (at + F)], plo_done)

            def l1_slot(g, half, e):
                if g >= 3:
                    add_l2(g - 3)
                if g + 2 < NG:
                    x1_lo(g + 2)
                piece_lo(e, half, 0, g + 1 + (2 if g > 1 else 0))
                if g == 1:
                    for w in range(2):
                        piece_lo(E3 - 1, w, F, 3 + w)
                if g == NG - 1:
                    x3_lo(0, 0)
                if g >= 1:
                    add_l1(g - 1)

            x1_lo(0)
            lo_part(0, TL0)
            x1_lo(1)
            for at in range(8):
                add_piece(0, TL0 + at)
            ve.wait_ge(bias_ok, 2)
            ve.wait_ge(y_added, TL0)
            for g in range(NG):
                l1_slot(g, g % 2, g // 2)

            def gate_columns(p):
                ve.wait_ge(s_out, 2 * p + 2)
                ve.tensor_copy(gS[:, :], ssb[:, bass.ds(p % 2 * 2, 2), :, 0:1].rearrange("p a j n -> p (a j n)")) \
                    .then_inc(gate_dve, 1)
                ve.wait_ge(gate_pe, 3 * p + 1)
                if isinstance(p, int) and p == NPAIR - 1:
                    for a, bank_ in enumerate((psX[0], psX[1])):
                        mm = ve.tensor_copy(gE[:, a * GB:(a + 1) * GB],
                                            bank_[:, :].rearrange("p (j n) -> p j n", j=GB)[:, :, 0])
                    mm.then_inc(gate_dve, 1)
                else:
                    ve.tensor_copy(gE[:, :], psX[1][:, 0:2 * GB]).then_inc(gate_dve, 1)

            def gate_relu(p):
                ve.wait_ge(gate_pe, 3 * p + 2)
                ve.tensor_scalar(ghid[:, :], psX[1][:, 8:8 + 2 * GB], 0.0, None, ALU.max).then_inc(gate_dve, 1)

            def gate_max(p):
                ve.wait_ge(gate_pe, 3 * p + 3)
                ve.tensor_copy(glog[:, :, :], psX[1][:, 16:16 + 4 * GB].rearrange("p (a b) -> p a b", a=2)) \
                    .then_inc(gate_dve, 1)
                ve.wait_ge(gate_dve, GATE_STEPS * p + 4)
                ve.tensor_tensor(gmax[:, :], glog[:, 0, :], glog[:, 1, :], ALU.max).then_inc(gate_dve, 1)
                ve.wait_ge(gate_dve, GATE_STEPS * p + 5)
                ve.tensor_tensor(gdiff[:, :, :], glog[:, :, :], gmax[:, :].unsqueeze(1).to_broadcast([P, 2, 2 * GB]),
                                 ALU.subtract).then_inc(gate_dve, 1)

            def gate_weights(p):
                both = [P, 2, 2 * GB]
                ve.wait_ge(gate_act, p + 1)
                ve.tensor_scalar(gnum[:, :, :], gtanh[:, :, :], 1.0, None, ALU.add).then_inc(gate_dve, 1)
                ve.tensor_scalar(gden[:, :, :], gtanh[:, :, :], -1.0, 1.0, ALU.mult, ALU.add).then_inc(gate_dve, 1)
                ve.wait_ge(gate_dve, GATE_STEPS * p + 8)
                for a in range(2):
                    ve.tensor_tensor(gexp[:, a, :], gnum[:, a, :], gden[:, 1 - a, :], ALU.mult) \
                        .then_inc(*((gate_dve, 1) if a else (gate_half, 1)))
                ve.wait_ge(gate_half, p + 1)
                ve.wait_ge(gate_dve, GATE_STEPS * p + 9)
                ve.tensor_tensor(gsum[:, :], gexp[:, 0, :], gexp[:, 1, :], ALU.add).then_inc(gate_dve, 1)
                ve.wait_ge(gate_dve, GATE_STEPS * p + 10)
                ve.reciprocal(grec[:, :], gsum[:, :]).then_inc(gate_dve, 1)
                ve.wait_ge(gate_dve, GATE_STEPS * p + 11)
                ve.tensor_tensor(gw[:, :, :], gexp[:, :, :], grec[:, :].unsqueeze(1).to_broadcast(both), ALU.mult) \
                    .then_inc(gate_dve, 1)
                ve.wait_ge(gate_dve, GATE_STEPS * p + 12)

            def of_pair(buf, p, a, j):
                return buf[:, bass.ds(p % 2 * 2 + a, 1), j, :].rearrange("p a n -> p (a n)")

            def mix_shared(p, a):
                reach(ve, z_ready, 2 * p)
                for j in range(GB):
                    n = a * GB + j
                    ve.scalar_tensor_tensor(out=z[:, a, j, :], in0=of_pair(ssb, p, a, j), scalar=gw[:, 1, n:n + 1],
                                            in1=xT[:, bass.ds(p * (2 * GT) + n * P, P)],
                                            op0=ALU.mult, op1=ALU.add).then_inc(z_done, 1)

            def mix_expert(p, a):
                ve.wait_ge(z_ready, 2 * p + a + 1)
                reach(ve, out_sem[a], 16 * p)
                for j in range(GB):
                    n = a * GB + j
                    ve.scalar_tensor_tensor(out=osb[:, a, j, :], in0=of_pair(esb, p, a, j), scalar=gw[:, 0, n:n + 1],
                                            in1=psX[1][:, j * P:(j + 1) * P],
                                            op0=ALU.mult, op1=ALU.add).then_inc(o_done, 1)

            def mix(p, half, k):
                if (half, k) == (0, 6):
                    gate_columns(p)
                if (half, k) == (0, 7):
                    gate_relu(p)
                if (half, k) == (1, 0):
                    gate_max(p)
                if (half, k) == (1, 2):
                    gate_weights(p)
                    mix_shared(p, 0)
                if (half, k) == (1, 3):
                    mix_shared(p, 1)
                if (half, k) == (1, 5):
                    mix_expert(p, 0)
                if (half, k) == (1, 7):
                    mix_expert(p, 1)

            def l3_slot(g, half, p=None):
                for k in range(8):
                    K = 8 * g + k
                    ve.wait_ge(gelu3, K + 1)
                    ve.wait_ge(u3, K + 1)
                    if k % 2 == 0:
                        reach(ve, slo, 4 * g + (k // 2 - 1))
                    else:
                        reach(ve, t_ready, 4 * g + (k // 2 - 1))
                    ve.tensor_tensor(hid[:, k % 4, :], act[:, k % 2, :], psU[k % 2][:, :], ALU.mult).then_inc(mul3, 1)
                    if k % 2 == 1:
                        ve.wait_ge(shi, 4 * g + (k // 2 + 1))
                        split_lo(shid(k // 2, 1), hid[:, (k - 1) % 4, :], shid(k // 2, 0), slo)
                    if isinstance(g, int) and g == 0 and k in after:
                        after[k]()
                    if p is not None:
                        mix(p, half, k)
                    if k == 3 and not (isinstance(g, int) and g == NG - 1):
                        x3_lo(g + 1, 1 - half)

            add_l2(NG - 3)
            after = {2: lambda: add_l2(NG - 2), 4: lambda: add_l1(NG - 1), 6: lambda: add_l2(NG - 1)}
            for half in range(2):
                l3_slot(half, half)
            with ve.Fori(1, NPAIR - 1) as p:
                for half in range(2):
                    l3_slot(2 * p + half, half, p - 1)
            for half in range(2):
                l3_slot(NG - 2 + half, half, NPAIR - 2)
            p = NPAIR - 1
            for a in range(2):
                ve.wait_ge(last_turned, a + 1)
                ve.tensor_copy(hid[:, 2 * a, :], psG[a][:, :]).then_inc(z_done, 1)
            gate_columns(p)
            gate_relu(p)
            gate_max(p)
            gate_weights(p)
            ve.wait_ge(last_turned, 4)
            ve.wait_ge(z_done, 8 * p + 2)
            for a in range(2):
                ve.wait_ge(out_sem[a], 16 * p)
                for j in range(GB):
                    n = a * GB + j
                    ve.scalar_tensor_tensor(out=part[:, a, j, :], in0=psU[a][:, j * P:(j + 1) * P],
                                            scalar=gw[:, 1, n:n + 1], in1=hid[:, 2 * a, j * P:(j + 1) * P],
                                            op0=ALU.mult, op1=ALU.add).then_inc(z_done, 1)
                ve.wait_ge(last_scaled, (a + 1) * GB)
                ve.wait_ge(z_done, 8 * p + 2 + (a + 1) * GB)
                ve.tensor_tensor(osb[:, a, :, :], part[:, a, :, :], last_e[:, a, :, :], ALU.add).then_inc(o_done, 1)

        @block.tensor
        def _(pe):
            def three(bank_, whi, wlo, mhi, mlo, start, stop):
                pe.matmul(bank_, whi, mhi, start=start, stop=False)
                pe.matmul(bank_, wlo, mhi, start=False, stop=False)
                return pe.matmul(bank_, whi, mlo, start=False, stop=stop)

            pe.wait_ge(ident_ok, 2)
            def x_turn(g):
                pe.wait_ge(x_in[g], 16)
                reach(pe, xt_done, g - 1)
                for j in range(GB):
                    mm = pe.transpose(psX[g % 2][:, j * P:(j + 1) * P], xtok[:, g * GB + j, :], ident[:, :])
                mm.then_inc(xt_ready, 1)

            def down(p, s):
                T, c, half = 64 * p + s, s % FC, (s - 4) // FC % 2
                dpar = (s - 4) // TILES % 2
                pe.wait_ge(lo_done, T - 3)
                if c == 0:
                    reach(pe, y_added, T - 8)
                three(psY[half][:, :], wset(dpar, 0, 2, c), wset(dpar, 1, 2, c),
                      ring(half, c, 0), ring(half, c, 1), c == 0, c == FC - 1).then_inc(d_done, 1)

            def slot(p, s, head=False):
                T, c, wpar, col = 64 * p + s, s % FC, s // TILES % 2, s % TILES // FC * GT
                for q, bank_, free, done in ((0, psG, silu_done, g_ready), (1, psU, mul_done, u_ready)):
                    reach(pe, free, T - 1)
                    whi, wlo = wset(wpar, 0, q, c), wset(wpar, 1, q, c)
                    if head and s == 0:
                        pe.wait_ge(*((sg_hi, 1) if q == 0 else (whi_done, 1)))
                        pe.wait_ge(xhi_done, 1)
                        pe.matmul(bank_[0][:, :], whi, xhi[:, 0:GT], start=True, stop=False)
                        pe.wait_ge(wlo_done, q + 1)
                        pe.matmul(bank_[0][:, :], wlo, xhi[:, 0:GT], start=False, stop=False)
                        pe.wait_ge(xlo_done, 1)
                        pe.matmul(bank_[0][:, :], whi, xlo[:, 0:GT], start=False, stop=True).then_inc(done, 1)
                        continue
                    three(bank_[c % 2][:, :], whi, wlo,
                          xhi[:, col:col + GT], xlo[:, col:col + GT], True, True).then_inc(done, 1)
                if not head or s >= 4:
                    down(p, s)

            def l1_weights(i):
                reach(pe, tr_done, i - 1)
                for c in range(FC):
                    if i < 4:
                        mm = pe.transpose(psX[i % 2][:, c * P:(c + 1) * P], exraw[:, i, c * P:(c + 1) * P],
                                          ident[:, :])
                    elif i == 4:
                        mm = pe.transpose(psX[0][:, c * SHARED:(c + 1) * SHARED], fc2raw[:, c * P:(c + 1) * P],
                                          ident[0:SHARED, 0:SHARED])
                    else:
                        mm = pe.transpose(psX[1][:, c * P:(c + 1) * P], fc1raw[:, c, :], ident[:, :])
                mm.then_inc(tr_ready, 1)

            x_turn(0)
            for t in range(TILES):
                if t % FC == 0 and t > 0:
                    pe.wait_ge(xlo_done, t // FC + 1)
                if t == FC:
                    pe.wait_ge(wlo_done, 3)
                slot(0, t, head=True)
                if t in X_TILE:
                    x_turn(X_TILE.index(t) + 1)
                if t == L1W_TILE[0]:
                    pe.wait_ge(l1w_in, 48)
                    pe.wait_ge(xt_done, NG)
                if t in L1W_TILE:
                    l1_weights(L1W_TILE.index(t))
            pe.wait_ge(hot_ok, 4)
            pe.wait_ge(tr_done, 6)
            pe.matmul(psX[0][:, 0:B], table1[:, :], hot[0:E1, 0, :], start=True, stop=True).then_inc(bias_ready, 1)
            pe.matmul(psX[1][:, 0:B], table2[:, :], hot[:, 1, :], start=True, stop=True).then_inc(bias_ready, 1)

            with pe.Fori(0, NE // 2) as p:
                for r in (1, 2):
                    pe.wait_ge(wlo_done, 6 * p + 3 * (r + 1))
                    for t in range(TILES):
                        slot(p, TILES * r + t)
            def l1_down(g, half, c):
                if c == 0:
                    pe.wait_ge(gelu_done, 4 * g + 4)
                    if isinstance(g, int) and g == 0:
                        pe.wait_ge(y_added, TL0)
                    else:
                        reach(pe, x2_done, 4 * g - 4)
                pe.wait_ge(w2_ready, 4 * g + (c + 1))
                for i in range(FC):
                    mm = pe.matmul(psY[half][:, c * P:(c + 1) * P], w2[:, half, c, i, :],
                                   h1[:, half, i, c * P:(c + 1) * P], start=i == 0, stop=i == FC - 1)
                mm.then_inc(l1_ready, 1)

            def l2(g, half, p):
                pe.wait_ge(x2_done, 4 * g + 4)
                pe.wait_ge(cat_in[half], 64 * p)
                for j in range(GB):
                    mm = pe.matmul(psX[half][:, j * P:(j + 1) * P], wcat[:, half, j, :],
                                   xT[:, bass.ds(g * GT + j * P, P)], start=True, stop=True)
                mm.then_inc(l2_ready, 1)

            def fc1(c):
                return fc1hi[:, c * P:(c + 1) * P], fc1lo[:, c * P:(c + 1) * P]

            def last_downs():
                pe.wait_ge(fc1lo_ok, 1)
                pe.wait_ge(x1hi, 1)
                for c in range(2):
                    pe.wait_ge(silu_done, TL0 - 1 + c)
                    for i in range(2):
                        pe.matmul(psG[c][:, :], fc1(c)[i], xhi[:, 0:GT], start=i == 0, stop=False)
                for c in range(FC):
                    down(0, TL0 + c)
                    if c < 2:
                        pe.wait_ge(x1lo, 1)
                        pe.matmul(psG[c][:, :], fc1(c)[0], xlo[:, 0:GT], start=False, stop=True).then_inc(fc_ready, 1)
                    else:
                        pe.wait_ge(gelu_done, c - 1)
                        three(psG[c % 2][:, :], *fc1(c), xhi[:, 0:GT], xlo[:, 0:GT], True, True).then_inc(fc_ready, 1)

            def l1_slot(g, half, p):
                for c in range(FC):
                    if c == 0:
                        pe.wait_ge(x1lo, g + 1)
                    reach(pe, gelu_done, 4 * g + (c - 1))
                    three(psG[c % 2][:, :], *fc1(c),
                          xhi[:, bass.ds(g * GT, GT)], xlo[:, bass.ds(g * GT, GT)], True, True) \
                        .then_inc(fc_ready, 1)
                    l1_down(g - 1, 1 - half, c)
                if not isinstance(g, int):
                    l2(g - 2, half, p)

            last_downs()
            pe.wait_ge(bias_ok, 2)
            pe.wait_ge(fc2_ok, 2 * GB - 1)
            l1_slot(1, 1, 0)
            with pe.Fori(1, NPAIR) as p:
                for half in range(2):
                    l1_slot(2 * p + half, half, p)
            def expert_of(g, j):
                return pe.value_load(idxs[0:1, 2, bass.ds(4 * g + j, 1)], min_val=0, max_val=E3 - 1)

            def expert_in(g, half, j):
                n = expert_of(g, j)
                mhi, mlo = xs_hi[:, half, j * P:(j + 1) * P], xs_lo[:, half, j * P:(j + 1) * P]
                for bank_, w, free, done in ((psG, 0, gelu3, g3), (psU, 1, mul3, u3)):
                    reach(pe, free, 8 * g + 2 * j)
                    whi = rbuf[:, bass.ds(n * EXP_STEP + (EXP_AT + w * 2 * F), F)]
                    wlo = rbuf[:, bass.ds(n * EXP_STEP + (EXP_AT + w * 2 * F + F), F)]
                    three(bank_[1][:, :], mhi, mlo, whi, wlo, True, True).then_inc(done, 1)

            def shared_in(g, half, c):
                for bank_, q, free, done in ((psG, 0, gelu3, g3), (psU, 1, mul3, u3)):
                    reach(pe, free, 8 * g + (2 * c - 1))
                    three(bank_[0][:, :], wset(1, 0, q, c), wset(1, 1, q, c), xs_hi[:, half, :], xs_lo[:, half, :],
                          True, True).then_inc(done, 1)

            def shared_down(g, c):
                pe.wait_ge(slo, 4 * g + (c + 1))
                if c == 0:
                    reach(pe, s_out, g)
                mm = three(psY[0][:, :], wset(1, 0, 2, c), wset(1, 1, 2, c), shid(c, 0), shid(c, 1),
                           c == 0, c == FC - 1)
                mm.then_inc(d_done, 1)

            def turn(g, j):
                pe.wait_ge(mul3, 8 * g + (2 * j + 2))
                reach(pe, t_out, 4 * g + j)
                for c in range(FC):
                    mm = pe.transpose(psX[0][:, c * P:(c + 1) * P], hid[:, (2 * j + 1) % 4, c * P:(c + 1) * P],
                                      ident[:, :])
                mm.then_inc(t_ready, 1)

            def expert_down(g, j):
                n = expert_of(g, j)
                pe.wait_ge(t_out, 4 * g + (j + 1))
                if j == 0:
                    reach(pe, e_out, g)
                for c in range(FC):
                    mm = pe.matmul(psY[1][:, j * P:(j + 1) * P], hT[:, j % 2, c * P:(c + 1) * P],
                                   woe[:, bass.ds(n, 1), c, :].rearrange("p a n -> p (a n)"),
                                   start=c == 0, stop=c == FC - 1)
                mm.then_inc(e_done, 1)

            def mix(p, half, k):
                if (half, k) == (0, 6):
                    pe.wait_ge(e0_in, 16 * p + 16)
                    reach(pe, o_done, 8 * p)
                    pe.matmul(psX[1][:, 0:2 * GB], e0r[:, :], ident[0:2 * GB, 0:2 * GB], start=True,
                              stop=True).then_inc(gate_pe, 1)
                if (half, k) == (0, 7):
                    pe.wait_ge(gate_dve, GATE_STEPS * p + 2)
                    pe.matmul(psX[1][:, 8:8 + 2 * GB], g0s[:, 1, :], gS[:, :], start=True, stop=False)
                    pe.matmul(psX[1][:, 8:8 + 2 * GB], g0s[:, 0, :], gE[:, :], start=False, stop=True) \
                        .then_inc(gate_pe, 1)
                if (half, k) == (1, 0):
                    pe.wait_ge(gate_dve, GATE_STEPS * p + 3)
                    for a in range(2):
                        mm = pe.matmul(psX[1][:, 16 + a * 2 * GB:16 + (a + 1) * 2 * GB], g1b[:, a, :], ghid[:, :],
                                       start=True, stop=True)
                    mm.then_inc(gate_pe, 1)
                for a in range(2):
                    if (half, k) == (1, 4 + 2 * a):
                        pe.wait_ge(z_done, 8 * p + (4 * a + 4))
                        reach(pe, o_done, 8 * p + 4 * a)
                        for j in range(GB):
                            mm = pe.transpose(psX[1][:, j * P:(j + 1) * P], z[:, a, j, :], ident[:, :])
                        mm.then_inc(z_ready, 1)

            def l3_slot(g, half, p=None, first=False, stream=True):
                for k in range(8):
                    if stream:
                        if k == 0:
                            pe.wait_ge(xslo, g + 1)
                        (expert_in if k % 2 else shared_in)(g, half, k // 2)
                        if first:
                            rest_of_l1(k)
                    late = not first or k >= 2
                    if k % 2 == 0 and late and (stream or k == 0):
                        shared_down(*((g, k // 2 - 1) if k else (g - 1, FC - 1)))
                    if k % 2 == 1:
                        if (not first or k >= 5) and (stream or k <= 3):
                            expert_down(*((g, k // 2 - 2) if k >= 5 else (g - 1, k // 2 + 2)))
                        if (not first or k >= 3) and (stream or k <= 1):
                            turn(*((g, k // 2 - 1) if k >= 3 else (g - 1, FC - 1)))
                    if p is not None:
                        mix(p, half, k)

            def rest_of_l1(k):
                if k < GB:
                    l1_down(NG - 1, 1, k)
                if k == 1:
                    l2(NG - 2, 0, NPAIR)
                    pe.wait_ge(x2_done, 4 * (NG - 1))
                if k == 3:
                    pe.wait_ge(x3_done, 4 * (NG - 1))
                if k == 5:
                    l2(NG - 1, 1, NPAIR)

            pe.wait_ge(plo_done, 2 * E3)
            pe.wait_ge(wo_in, 16 * E3)
            pe.wait_ge(gelu_done, TILES)
            pe.wait_ge(g1b_ok, 2)
            l3_slot(0, 0, first=True)
            l3_slot(1, 1)
            with pe.Fori(1, NPAIR - 1) as p:
                for half in range(2):
                    l3_slot(2 * p + half, half, p - 1)
            for half in range(2):
                l3_slot(NG - 2 + half, half, NPAIR - 2)
            def turn_last(bank_, src):
                for j in range(GB):
                    mm = pe.transpose(bank_[:, j * P:(j + 1) * P], src(j), ident[:, :])
                return mm

            p = NPAIR - 1
            shared_down(NG - 1, FC - 1)
            expert_down(NG - 1, 2)
            turn(NG - 1, GB - 1)
            pe.wait_ge(gelu3, 8 * NG)
            for a in range(2):
                turn_last(psG[a], lambda j: xT[:, (8 * p + a * GB + j) * P:(8 * p + a * GB + j + 1) * P]) \
                    .then_inc(last_turned, 1)
            expert_down(NG - 1, GB - 1)
            pe.wait_ge(mul3, 8 * NG)
            pe.wait_ge(s_out, NG)
            for a in range(2):
                turn_last(psU[a], lambda j: ssb[:, LAST_RING + a, j, :]).then_inc(last_turned, 1)
            pe.wait_ge(o_done, 8 * p)
            for a in range(2):
                pe.wait_ge(e_out, NG - 1 + a)
                mm = turn_last(psX[a], lambda j: esb[:, LAST_RING + a, j, :])
            mm.then_inc(gate_pe, 1)
            mix(p, 0, 7)
            mix(p, 1, 0)


_INS = ['x', 'fside_Bx8_0', 'condB_sharedgateprob', 'itok_B_0_15', 'itok_B_0_63', 'itok_B_0_2',
        'L0_cond_Wg', 'L0_cond_Wu', 'L0_cond_Wd', 'L0_cond_Sg', 'L0_cond_Su', 'L0_cond_Sd',
        'L1_cond_fc1_w', 'L1_cond_fc1_b', 'L1_cond_fc2_w', 'L1_cond_fc2_b', 'L1_cond_experts_w', 'L1_cond_experts_b',
        'L2_cond_W', 'L2_cond_b', 'L3_cond_Wi0', 'L3_cond_Wi1', 'L3_cond_Wo',
        'L3_cond_sWi0', 'L3_cond_sWi1', 'L3_cond_sWo', 'L3_cond_g0', 'L3_cond_g1']


def kernel(**inputs):
    import numpy as np
    import concourse.bacc as bacc
    from concourse import mybir as mb
    from concourse.bass_utils import run_bass_kernel_spmd

    nc = bacc.Bacc("TRN2", target_bir_lowering=False, num_devices=1)
    arrays, args = {}, []
    for name in _INS:
        a = np.ascontiguousarray(inputs[name])
        arrays[f"in_{name}"] = a
        args.append(nc.dram_tensor(f"in_{name}", a.shape, mb.dt.from_np(a.dtype), kind="ExternalInput").ap())
    result = nc.dram_tensor("out_x", (B, P, P), mb.dt.float32, kind="ExternalOutput").ap()
    build_kernel(nc, *args, result)
    r = run_bass_kernel_spmd(nc, [arrays], core_ids=[0])
    return r.results[0]["out_x"]
```

```python
from contextlib import ExitStack

import concourse.bass as bass
from concourse import mybir

F32 = mybir.dt.float32
F32R = mybir.dt.float32r
I32 = mybir.dt.int32
ALU = mybir.AluOpType
ACT = mybir.ActivationFunctionType

P = 128
B = 32
GB = 4
GT = GB * P
NG = B // GB
NPAIR = NG // 2
FC = 4
F = FC * P
NE = 8
ROUNDS = NE + 1
E1 = 16
PART = 32
SHARED = P - PART
E2 = 64
E3 = 5
WSET = 3 * F
TILES = NG * FC
WARM_UP = (7, 6)
X_TILE = [3 * g for g in range(NG - 1)]
X_HI_TILE = [0] + [t + 1 for t in X_TILE[1:]]
L1W_TILE = [19 + 2 * i for i in range(6)]

SET_AT = [2 * WSET, 0]
RING_AT = 4 * WSET
EXP_AT = 2 * WSET
EXP_STEP = 4 * F
RBUF = RING_AT + 2 * FC * 2 * GT
LAST_RING = (NPAIR - 1) % 2 * 2
GATE_STEPS = 12


def reach(eng, sem, value):
    if isinstance(value, int) and value <= 0:
        return
    eng.wait_ge(sem, value)


def build_kernel(nc, x, fside, sgate, idx1, idx2, idx3, Wg, Wu, Wd, Sg, Su, Sd,
                 fc1_w, fc1_b, fc2_w, fc2_b, ex_w, ex_b, W2, b2,
                 Wi0, Wi1, Wo, sWi0, sWi1, sWo, g0, g1, out):
    with ExitStack() as ctx:
        def sb(name, shape, dt=F32):
            return ctx.enter_context(nc.sbuf_tensor(name, shape, dt))

        def bank(name):
            return ctx.enter_context(nc.psum_tensor(name, [P, GT], F32))

        def sem(name):
            return ctx.enter_context(nc.semaphore(name))

        psG = [bank("psG0"), bank("psG1")]
        psU = [bank("psU0"), bank("psU1")]
        psY = [bank("psY0"), bank("psY1")]
        psX = [bank("psX0"), bank("psX1")]

        xT = sb("xT", [P, B * P])
        xhi = sb("xhi", [P, B * P], F32R)
        xlo = sb("xlo", [P, B * P], F32R)
        rbuf = sb("rbuf", [P, RBUF], F32R)
        raw = sb("raw", [P, 2, WSET])
        act = sb("act", [P, 2, GT])
        hid = sb("hid", [P, 4, GT])
        h1 = sb("h1", [P, 2, FC, GT])
        ident = sb("ident", [P, P])
        gates = sb("gates", [P, ROUNDS * B])
        fs = sb("fs", [P, B * NE])
        omg = sb("omg", [P, B])
        fc1hi = sb("fc1hi", [P, F], F32R)
        fc1lo = sb("fc1lo", [P, F], F32R)
        fc1T = sb("fc1T", [P, F])
        fc1b = sb("fc1b", [P, FC])
        exT = sb("exT", [P, E1, FC, PART])
        w2 = sb("w2", [P, 2, GB, FC, P])
        bias1 = sb("bias1", [P, B])
        bias2 = sb("bias2", [P, B])
        idxs = sb("idxs", [1, 3, B], I32)
        hot = sb("hot", [E2, 2, B])
        wcat = sb("wcat", [P, 2, GB, P])
        woe = sb("woe", [P, E3, FC, P])
        g1b = sb("g1b", [P, 2, P])
        g0s = sb("g0s", [P, 2, P])
        xs_hi = sb("xs_hi", [P, 2, GT], F32R)
        xs_lo = sb("xs_lo", [P, 2, GT], F32R)
        idxb = sb("idxb", [E2, 2, B], I32)
        idxf = sb("idxf", [E2, 2, B])
        row_id = sb("row_id", [E2, 1], I32)
        row_f = sb("row_f", [E2, 1])
        table1 = sb("table1", [E1, P])
        table2 = sb("table2", [E2, P])
        e0r = sb("e0r", [2 * GB, P])
        g1s = sb("g1s", [P, 2])
        gE = sb("gE", [P, 2 * GB])
        gS = sb("gS", [P, 2 * GB])
        ghid = sb("ghid", [P, 2 * GB])
        glog = sb("glog", [P, 2, 2 * GB])
        gmax = sb("gmax", [P, 2 * GB])
        gdiff = sb("gdiff", [P, 2, 2 * GB])
        gtanh = sb("gtanh", [P, 2, 2 * GB])
        gnum = sb("gnum", [P, 2, 2 * GB])
        gden = sb("gden", [P, 2, 2 * GB])
        gexp = sb("gexp", [P, 2, 2 * GB])
        gsum = sb("gsum", [P, 2 * GB])
        grec = sb("grec", [P, 2 * GB])
        gw = sb("gw", [P, 2, 2 * GB])

        h1f = h1[:, :, :, :].rearrange("p a c n -> p (a c n)")
        xtok = h1f.rearrange("p (b d) -> p b d", b=B)
        hT = h1f[:, 0:2 * F].rearrange("p (a n) -> p a n", a=2)
        esb = h1f[:, 2 * F:6 * F].rearrange("p (a j n) -> p a j n", a=2 * 2, j=GB)
        osb = h1f[:, 6 * F:8 * F].rearrange("p (a j n) -> p a j n", a=2, j=GB)
        w2f = w2[:, :, :, :, :].rearrange("p a j c n -> p (a j c n)")
        z = w2f[:, 0:2 * GT].rearrange("p (a j n) -> p a j n", a=2, j=GB)
        part = z
        last_e = w2f[:, 6 * GT:8 * GT].rearrange("p (a j n) -> p a j n", a=2, j=GB)
        ssb = w2f[:, 2 * GT:6 * GT].rearrange("p (a j n) -> p a j n", a=2 * 2, j=GB)
        exraw = woe[:, :, :, :].rearrange("p e c n -> p (e c n)")[:, 0:4 * F].rearrange("p (r f) -> p r f", r=4)
        fc2raw = wcat[0:SHARED, 0, :, :].rearrange("p j n -> p (j n)")
        fc1raw = wcat[:, 1, :, :]

        def wset(par, lo, q, c):
            at = SET_AT[par] + lo * WSET + q * F + c * P
            return rbuf[:, at:at + P]

        def shid(c, lo):
            return (xlo if lo else xhi)[:, c * GT:(c + 1) * GT]

        def ring(half, c, lo):
            at = RING_AT + (half * FC + c) * 2 * GT + lo * GT
            return rbuf[:, at:at + GT]

        x0_in = [sem("x0_in0"), sem("x0_in1")]
        x_in = [sem(f"x_in{g}") for g in range(NG)]
        small_in, idx_in, l1w_in, g_in = sem("small_in"), sem("idx_in"), sem("l1w_in"), sem("g_in")
        first_in = [sem("first_in0"), sem("first_in1"), sem("first_in2")]
        raw_in = [sem("raw_in0"), sem("raw_in1")]
        cat_in = [sem("cat_in0"), sem("cat_in1")]
        wo_in, e0_in, out_sem = sem("wo_in"), sem("e0_in"), [sem("out_sem0"), sem("out_sem1")]
        ident_ok, hot_ok = sem("ident_ok"), sem("hot_ok")
        xt_ready, xt_done, xhi_done, xlo_done = sem("xt_ready"), sem("xt_done"), sem("xhi_done"), sem("xlo_done")
        sg_hi, gates_ok, g1b_ok = sem("sg_hi"), sem("gates_ok"), sem("g1b_ok")
        tr_ready, tr_done, fc1hi_ok, fc1lo_ok, fc2_ok = (sem("tr_ready"), sem("tr_done"), sem("fc1hi_ok"),
                                                         sem("fc1lo_ok"), sem("fc2_ok"))
        bias_ready, bias_ok = sem("bias_ready"), sem("bias_ok")
        whi_done, wlo_done = sem("whi_done"), sem("wlo_done")
        g_ready, u_ready, d_done = sem("g_ready"), sem("u_ready"), sem("d_done")
        silu_done, mul_done, hi_done, lo_done, y_added = (sem("silu_done"), sem("mul_done"), sem("hi_done"),
                                                          sem("lo_done"), sem("y_added"))
        fc_ready, gelu_done, l1_ready, l2_ready = sem("fc_ready"), sem("gelu_done"), sem("l1_ready"), sem("l2_ready")
        x1_first, x1hi, x1lo, x2_done, x3_done = (sem("x1_first"), sem("x1hi"), sem("x1lo"), sem("x2_done"),
                                                  sem("x3_done"))
        w2_ready = sem("w2_ready")
        p_in, last_in = [sem("p_in0"), sem("p_in1")], sem("last_in")
        phi_done, plo_done = sem("phi_done"), sem("plo_done")
        xshi, xslo = sem("xshi"), sem("xslo")
        g3, u3, gelu3, mul3 = sem("g3"), sem("u3"), sem("gelu3"), sem("mul3")
        shi, slo, s_out = sem("shi"), sem("slo"), sem("s_out")
        t_ready, t_out, e_done, e_out = sem("t_ready"), sem("t_out"), sem("e_done"), sem("e_out")
        gate_pe, gate_dve, gate_half, gate_act = (sem("gate_pe"), sem("gate_dve"), sem("gate_half"),
                                                  sem("gate_act"))
        last_scaled, last_turned, last_x3 = sem("last_scaled"), sem("last_turned"), sem("last_x3")
        z_done, z_ready, o_done = sem("z_done"), sem("z_ready"), sem("o_done")

        TL0 = ROUNDS * TILES

        block = ctx.enter_context(nc.Block())

        @block.sync
        def _(sp):
            def load_raw(par, gate, up, down, free):
                if free is not None:
                    sp.wait_ge(wlo_done, free)
                for q, w in ((0, gate), (1, up)):
                    sp.dma_start(raw[:, par, q * F:(q + 1) * F], w).then_inc(raw_in[par], 16)
                sp.dma_start(raw[:, par, 2 * F:3 * F].rearrange("p (c d) -> p c d", c=FC),
                             down.rearrange("(c p) d -> p c d", p=P)).then_inc(raw_in[par], 16)

            def load_x(g):
                sp.dma_start(xtok[:, g * GB:(g + 1) * GB, :],
                             x[g * GB:(g + 1) * GB].rearrange("b n d -> n b d")).then_inc(x_in[g], 16)

            for i in range(2):
                sp.dma_start(xtok[:, 2 * i:2 * i + 2, :], x[2 * i:2 * i + 2].rearrange("b n d -> n b d")) \
                    .then_inc(x0_in[i], 16)
            sp.dma_start(raw[:, 0, 0:F], Sg).then_inc(first_in[0], 16)
            sp.dma_start(raw[:, 0, F:2 * F], Su).then_inc(first_in[1], 16)
            load_x(1)
            sp.dma_start(raw[:, 0, 2 * F:3 * F].rearrange("p (c d) -> p c d", c=FC),
                         Sd.rearrange("(c p) d -> p c d", p=P)).then_inc(first_in[2], 16)
            load_x(2)
            sp.dma_start(gates[:, 0:B], sgate.partition_broadcast(P)).then_inc(small_in, 16)
            sp.dma_start(fs[:, :], fside.rearrange("b e -> (b e)").partition_broadcast(P)).then_inc(small_in, 16)
            for g in range(3, NG):
                load_x(g)
            load_raw(1, Wg[0], Wu[0], Wd[0], None)
            sp.dma_start(exraw, ex_w.rearrange("e p f -> (e p) f").rearrange("(r q) f -> q r f", q=P)) \
                .then_inc(l1w_in, 16)
            sp.dma_start(fc2raw, fc2_w).then_inc(l1w_in, 16)
            sp.dma_start(fc1raw, fc1_w.rearrange("(c q) d -> q c d", q=P)).then_inc(l1w_in, 16)
            sp.dma_start(idxb[:, 0, :], idx1.partition_broadcast(E2)).then_inc(g_in, 16)
            sp.dma_start(idxb[:, 1, :], idx2.partition_broadcast(E2)).then_inc(g_in, 16)
            sp.dma_start(table1[:, SHARED:P], ex_b).then_inc(g_in, 16)
            sp.dma_start(table1[:, 0:SHARED], fc2_b.partition_broadcast(E1)).then_inc(g_in, 16)
            sp.dma_start(table2[:, :], b2).then_inc(g_in, 16)
            with nc.allow_non_contiguous_dma(reason="128 x 4 and 128 x 2 numbers"):
                sp.dma_start(fc1b[:, :], fc1_b.rearrange("(c p) -> p c", p=P)).then_inc(g_in, 16)
                sp.dma_start(g1s[:, :], g1).then_inc(g_in, 16)
            sp.dma_start(g0s[:, :, :], g0.rearrange("(a p) d -> p a d", p=P)).then_inc(g_in, 16)
            sp.dma_start(idxs[0:1, 0, :], idx1.rearrange("(a b) -> a b", a=1)).then_inc(idx_in, 16)
            sp.dma_start(idxs[0:1, 1, :], idx2.rearrange("(a b) -> a b", a=1)).then_inc(idx_in, 16)
            sp.dma_start(idxs[0:1, 2, :], idx3.rearrange("(a b) -> a b", a=1)).then_inc(idx_in, 16)
            with sp.Fori(1, NPAIR) as p:
                load_raw(0, Wg[bass.ds(2 * p - 1, 1)].rearrange("a d f -> (a d) f"),
                         Wu[bass.ds(2 * p - 1, 1)].rearrange("a d f -> (a d) f"),
                         Wd[bass.ds(2 * p - 1, 1)].rearrange("a d f -> (a d) f"), 6 * p - 3)
                load_raw(1, Wg[bass.ds(2 * p, 1)].rearrange("a d f -> (a d) f"),
                         Wu[bass.ds(2 * p, 1)].rearrange("a d f -> (a d) f"),
                         Wd[bass.ds(2 * p, 1)].rearrange("a d f -> (a d) f"), 6 * p)
            load_raw(0, Wg[NE - 1], Wu[NE - 1], Wd[NE - 1], 3 * (ROUNDS - 2))
            load_raw(1, sWi0, sWi1, sWo, 3 * (ROUNDS - 1))
            sp.wait_ge(tr_done, 6)
            for e in range(E3):
                sp.dma_start(woe[:, e, :, :], Wo[e].rearrange("(c p) d -> p c d", p=P)).then_inc(wo_in, 16)

            def load_cat(b, half, j):
                n = sp.value_load(idxs[0:1, 1, b], min_val=0, max_val=E2 - 1)
                sp.dma_start(wcat[:, half, j, :], W2[bass.ds(n, 1)].rearrange("a d h -> (a d) h")) \
                    .then_inc(cat_in[half], 16)

            def load_piece(half, e, free):
                if free is not None:
                    sp.wait_ge(plo_done, free)
                w = (Wi0, Wi1)[half]
                src = w[e] if isinstance(e, int) else w[bass.ds(e, 1)].rearrange("a d f -> (a d) f")
                sp.dma_start(raw[:, half, 0:F], src).then_inc(p_in[half], 16)

            sp.wait_ge(idx_in, 48)
            for half in range(2):
                for j in range(GB):
                    load_cat(bass.ds(half * GB + j, 1), half, j)
            sp.wait_ge(wlo_done, 3 * (ROUNDS + 1))
            for half in range(2):
                load_piece(half, 0, None)
            for half in range(2):
                sp.dma_start(raw[:, half, F:2 * F], (Wi0, Wi1)[half][E3 - 1]).then_inc(last_in, 16)
            def load_cats(p, half):
                sp.wait_ge(l2_ready, 2 * p + half - 1)
                for j in range(GB):
                    load_cat(bass.ds(8 * p + (half * GB + j), 1), half, j)

            for half in range(2):
                load_piece(half, 1, half + 3)
            with sp.Fori(1, NPAIR - 1) as p:
                for half in range(2):
                    load_cats(p, half)
                    load_piece(half, p + 1, 2 * p + half + 3)
            for half in range(2):
                load_cats(NPAIR - 1, half)

            def finish_pair(p):
                sp.wait_ge(e_out, 2 * p + 2)
                sp.dma_start(e0r[:, :], esb[0:1, bass.ds(p % 2 * 2, 2), :, :].rearrange("o a j n -> o (a j) n")) \
                    .then_inc(e0_in, 16)
                for half in range(2):
                    sp.wait_ge(o_done, 2 * GB * p + GB * (half + 1))
                    sp.dma_start(out[bass.ds(8 * p + half * GB, GB)].rearrange("b n d -> n b d"),
                                 osb[:, half, :, :]).then_inc(out_sem[half], 16)

            with sp.Fori(0, NPAIR - 1) as p:
                finish_pair(p)
            for i in range(4):
                sp.wait_ge(o_done, 2 * GB * (NPAIR - 1) + i + 1)
                b0 = B - 2 * GB + 2 * i
                sp.dma_start(out[b0:b0 + 2].rearrange("b n d -> n b d"),
                             osb[:, i // 2, i % 2 * 2:i % 2 * 2 + 2, :]).then_inc(out_sem[i // 2], 16)
            for half in range(2):
                sp.wait_ge(out_sem[half], 16 * (NPAIR + 1))

        @block.gpsimd
        def _(pool):
            pool.memset(ident[:, :], 0.0).then_inc(ident_ok, 1)
            pool.wait_ge(ident_ok, 1)
            pool.affine_select(out=ident[:, :], in_=ident[:, :], compare_op=ALU.not_equal, fill=1.0, base=0,
                               pattern=[[-1, P]], channel_multiplier=1).then_inc(ident_ok, 1)
            pool.iota(row_id[:, :], pattern=[[0, 1]], base=0, channel_multiplier=1).then_inc(hot_ok, 1)
            pool.wait_ge(tr_done, 5)
            for s in range(1, 2 * GB):
                pool.tensor_copy(w2[:, s // GB, s % GB, :, 0:SHARED], w2[:, 0, 0, :, 0:SHARED]).then_inc(fc2_ok, 1)
            pool.wait_ge(tr_done, 6)
            pool.wait_ge(idx_in, 48)

            def expert_columns(b, half, j, free):
                n = pool.value_load(idxs[0:1, 0, b], min_val=0, max_val=E1 - 1)
                if free is not None:
                    pool.wait_ge(l1_ready, free)
                pool.tensor_copy(w2[:, half, j, :, SHARED:P],
                                 exT[:, bass.ds(n, 1), :, :].rearrange("p a c n -> p (a c) n")).then_inc(w2_ready, 1)

            for s in range(2 * GB):
                expert_columns(bass.ds(s, 1), s // GB, s % GB, None)
            pool.wait_ge(y_added, TL0 - TILES + 4)
            pool.wait_ge(u_ready, TL0 - TILES + 4)
            pool.tensor_copy(xhi[:, 0:GT], xT[:, 0:GT]).then_inc(x1_first, 1)
            pool.wait_ge(x1_first, 1)
            pool.tensor_tensor(xlo[:, 0:GT], xT[:, 0:GT], xhi[:, 0:GT].bitcast(F32), ALU.subtract) \
                .then_inc(x1_first, 1)
            with pool.Fori(1, NPAIR) as p:
                for s in range(2 * GB):
                    expert_columns(bass.ds(8 * p + s, 1), s // GB, s % GB, 8 * p + (s - 7))

        @block.scalar
        def _(sc):
            def x0_hi(i):
                sc.wait_ge(xt_done, i + 1)
                sc.activation(xhi[:, 2 * i * P:2 * (i + 1) * P], xT[:, 2 * i * P:2 * (i + 1) * P], ACT.Copy) \
                    .then_inc(xhi_done, 1)

            def x_hi(g):
                sc.wait_ge(xt_done, g + 2)
                sc.activation(xhi[:, g * GT:(g + 1) * GT], xT[:, g * GT:(g + 1) * GT], ACT.Copy).then_inc(xhi_done, 1)

            def first_hi(q):
                sc.wait_ge(first_in[q], 16)
                sc.activation(rbuf[:, SET_AT[0] + q * F:SET_AT[0] + (q + 1) * F], raw[:, 0, q * F:(q + 1) * F],
                              ACT.Copy).then_inc(whi_done, 1)

            def slot(p, s, hi=True, gu=True):
                T, c = 64 * p + s, s % FC
                if gu:
                    sc.wait_ge(g_ready, T + 1)
                    reach(sc, mul_done, T - 1)
                    sc.activation(act[:, c % 2, :], psG[c % 2][:, :], ACT.Silu).then_inc(silu_done, 1)
                if hi:
                    sc.wait_ge(mul_done, T)
                    reach(sc, d_done, T - 8)
                    k = (s - 1) % FC
                    sc.activation(ring((s - 1) // FC % 2, k, 0), hid[:, k, :], ACT.Copy).then_inc(hi_done, 1)

            def split_third(p, r, third):
                par = (r + 1) % 2
                sc.wait_ge(raw_in[par], 48 * p + 48 * ((r + 1 + par) // 2))
                reach(sc, d_done, 64 * p + TILES * r)
                at = SET_AT[par] + third * F
                sc.activation(rbuf[:, at:at + F], raw[:, par, third * F:(third + 1) * F], ACT.Copy) \
                    .then_inc(whi_done, 1)

            def round_(p, r):
                for t in range(TILES):
                    s = TILES * r + t
                    slot(p, s, hi=s > 0)
                    if r == 0 and t in X_HI_TILE:
                        x_hi(X_HI_TILE.index(t) + 1)
                    if t % 8 == 1 and t > 8:
                        split_third(p, r, t // 8 - 1)

            sc.wait_ge(ident_ok, 2)
            sc.activation(act[0:1, 0, 0:1], ident[0:1, 0:1], ACT.Silu)
            for i in range(2):
                x0_hi(i)
            for q in (1, 2):
                first_hi(q)
            round_(0, 0)
            sc.wait_ge(tr_done, 6)
            sc.activation(fc1hi[:, :], fc1T[:, :], ACT.Copy).then_inc(fc1hi_ok, 1)
            with sc.Fori(0, NE // 2) as p:
                for r in (1, 2):
                    round_(p, r)

            def split_x1(g):
                sc.wait_ge(y_added, 4 * g + (TL0 - TILES + 4))
                sc.wait_ge(u_ready, 4 * g + (TL0 - TILES + 4))
                sc.activation(xhi[:, bass.ds(g * GT, GT)], xT[:, bass.ds(g * GT, GT)], ACT.Copy).then_inc(x1hi, 1)

            def l1_slot(g, half, e, last_expert=False):
                for c in range(FC):
                    sc.wait_ge(fc_ready, 4 * g + (c + 1))
                    if c == 0:
                        reach(sc, l1_ready, 4 * g - 4)
                    sc.activation(h1[:, half, c, :], psG[c % 2][:, :], ACT.Gelu, bias=fc1b[:, c:c + 1]) \
                        .then_inc(gelu_done, 1)
                    if c == (3 if isinstance(g, int) and g == 0 else 1):
                        sc.wait_ge(p_in[half], 16 * e + 16)
                        sc.wait_ge(d_done, TL0)
                        at = EXP_AT + half * 2 * F
                        sc.activation(rbuf[:, bass.ds(e * EXP_STEP + at, F)], raw[:, half, 0:F], ACT.Copy) \
                            .then_inc(phi_done, 1)
                    if c == 3 and (not isinstance(g, int) or g + 2 < NG):
                        split_x1(g + 2)
                if last_expert:
                    for w in range(2):
                        sc.wait_ge(last_in, 32)
                        at = EXP_AT + (E3 - 1) * EXP_STEP + w * 2 * F
                        sc.activation(rbuf[:, at:at + F], raw[:, w, F:2 * F], ACT.Copy).then_inc(phi_done, 1)

            sc.wait_ge(g_in, 16 * 8)
            slot(0, TL0, gu=False)
            split_x1(1)
            for half in range(2):
                l1_slot(half, half, 0, last_expert=half == 1)
            with sc.Fori(1, NPAIR - 1) as p:
                for half in range(2):
                    l1_slot(2 * p + half, half, p)

            def split_x3(g, half):
                sc.wait_ge(x3_done, 4 * g + 4)
                reach(sc, u3, 8 * g - 8)
                sc.activation(xs_hi[:, half, :], xT[:, bass.ds(g * GT, GT)], ACT.Copy).then_inc(xshi, 1)

            l1_slot(NG - 2, 0, NPAIR - 1)
            split_x3(0, 0)
            l1_slot(NG - 1, 1, NPAIR - 1)

            def shared_hi(g, c):
                sc.wait_ge(mul3, 8 * g + (2 * c + 2))
                reach(sc, d_done, 4 * g + (c - 3 + TL0))
                sc.activation(shid(c, 0), hid[:, (2 * c + 1) % 4, :], ACT.Copy).then_inc(shi, 1)

            def turned_out(g, j):
                sc.wait_ge(t_ready, 4 * g + (j + 1))
                reach(sc, e_done, 4 * g + (j - 1))
                sc.activation(hT[:, j % 2, :], psX[0][:, :], ACT.Copy).then_inc(t_out, 1)

            def shared_out(g):
                sc.wait_ge(d_done, 4 * g + (TL0 + 4))
                sc.activation(ssb[:, bass.ds(g % 4, 1), :, :].rearrange("p a j n -> p (a j n)"),
                              psY[0][:, :], ACT.Copy).then_inc(s_out, 1)

            def expert_out(g):
                sc.wait_ge(e_done, 4 * g + 4)
                sc.activation(esb[:, bass.ds(g % 4, 1), :, :].rearrange("p a j n -> p (a j n)"),
                              psY[1][:, :], ACT.Copy).then_inc(e_out, 1)

            def l3_slot(g, half, first=False, last=False, mix=None):
                for k in range(8):
                    K = 8 * g + k
                    sc.wait_ge(g3, K + 1)
                    reach(sc, mul3, K - 1)
                    sc.activation(act[:, k % 2, :], psG[k % 2][:, :], ACT.Gelu_apprx_tanh).then_inc(gelu3, 1)
                    if k % 2 == 0 and (not first or k >= 2):
                        shared_hi(*((g, k // 2 - 1) if k else (g - 1, FC - 1)))
                    if k % 2 == 1 and (not first or k >= 3):
                        turned_out(*((g, k // 2 - 1) if k >= 3 else (g - 1, GB - 1)))
                    if k == 1 and mix is not None:
                        gate_tanh(mix)
                    if k == 2 and not first:
                        shared_out(g - 1)
                    if k == 3 and not first:
                        expert_out(g - 1)
                    if k == 4 and not last:
                        split_x3(g + 1, 1 - half)

            def gate_tanh(p):
                sc.wait_ge(gate_dve, GATE_STEPS * p + 6)
                sc.activation(gtanh[:, :, :], gdiff[:, :, :], ACT.Tanh, scale=0.5).then_inc(gate_act, 1)

            l3_slot(0, 0, first=True)
            l3_slot(1, 1)
            with sc.Fori(1, NPAIR - 1) as p:
                l3_slot(2 * p, 0)
                l3_slot(2 * p + 1, 1, mix=p - 1)
            l3_slot(NG - 2, 0)
            l3_slot(NG - 1, 1, last=True, mix=NPAIR - 2)
            turned_out(NG - 1, GB - 1)
            shared_hi(NG - 1, FC - 1)
            expert_out(NG - 1)
            shared_out(NG - 1)
            for a in range(2):
                sc.wait_ge(last_turned, 3 + a)
                sc.wait_ge(slo, FC * NG)
                sc.activation(hid[:, 2 * a + 1, :], psG[a][:, :], ACT.Copy).then_inc(last_x3, 1)
                if a == 0:
                    gate_tanh(NPAIR - 1)
            sc.wait_ge(gate_dve, GATE_STEPS * NPAIR)
            for n in range(2 * GB):
                sc.activation(last_e[:, n // GB, n % GB, :], esb[:, LAST_RING + n // GB, n % GB, :], ACT.Identity,
                              scale=gw[:, 0, n:n + 1]).then_inc(last_scaled, 1)

        @block.vector
        def _(ve):
            def split_lo(dst, value, hi, done):
                ve.tensor_tensor(dst, value, hi.bitcast(F32), ALU.subtract).then_inc(done, 1)

            def x0_out(i):
                ve.wait_ge(xt_ready, i + 1)
                ve.tensor_copy(xT[:, 2 * i * P:2 * (i + 1) * P], (psX[0], psY[0])[i][:, 0:2 * P]).then_inc(xt_done, 1)

            def x0_lo(i):
                ve.wait_ge(xhi_done, i + 1)
                ve.wait_ge(xt_done, i + 1)
                at = slice(2 * i * P, 2 * (i + 1) * P)
                split_lo(xlo[:, at], xT[:, at], xhi[:, at], xlo_done)

            def x_out(g):
                ve.wait_ge(xt_ready, g + 2)
                ve.tensor_copy(xT[:, g * GT:(g + 1) * GT], psX[g % 2][:, :]).then_inc(xt_done, 1)

            def x_lo(g):
                ve.wait_ge(xhi_done, g + 2)
                ve.wait_ge(xt_done, g + 2)
                split_lo(xlo[:, g * GT:(g + 1) * GT], xT[:, g * GT:(g + 1) * GT], xhi[:, g * GT:(g + 1) * GT],
                         xlo_done)

            def first_lo(q):
                ve.wait_ge(*((whi_done, q) if q else (sg_hi, 1)))
                ve.wait_ge(first_in[q], 16)
                split_lo(rbuf[:, SET_AT[0] + WSET + q * F:SET_AT[0] + WSET + (q + 1) * F],
                         raw[:, 0, q * F:(q + 1) * F], rbuf[:, SET_AT[0] + q * F:SET_AT[0] + (q + 1) * F], wlo_done)

            def weigh():
                ve.wait_ge(small_in, 32)
                ve.tensor_scalar(omg[:, :], gates[:, 0:B], -1.0, 1.0, ALU.mult, ALU.add).then_inc(gates_ok, 1)
                ve.wait_ge(gates_ok, 1)
                ve.tensor_tensor(gates[:, B:ROUNDS * B].rearrange("p (e b) -> p e b", e=NE),
                                 fs[:, :].rearrange("p (b e) -> p e b", e=NE),
                                 omg[:, :].unsqueeze(1).to_broadcast([P, NE, B]), ALU.mult).then_inc(gates_ok, 1)

            def add_piece(p, s):
                T, c = 64 * p + s, s % FC
                ve.wait_ge(d_done, T - (8 - FC) - c)
                xb = xT[:, (s - 8) % B * P:((s - 8) % B + 1) * P]
                ve.scalar_tensor_tensor(out=xb, in0=psY[s // FC % 2][:, c * P:(c + 1) * P],
                                        scalar=gates[:, bass.ds(T - 8, 1)], in1=xb,
                                        op0=ALU.mult, op1=ALU.add).then_inc(y_added, 1)

            def lo_part(p, s):
                T, k, half = 64 * p + s, (s - 1) % FC, (s - 1) // FC % 2
                ve.wait_ge(hi_done, T)
                ve.wait_ge(mul_done, T)
                reach(ve, d_done, T - 8)
                split_lo(ring(half, k, 1), hid[:, k, :], ring(half, k, 0), lo_done)

            def slot(p, s, head=False):
                T, c = 64 * p + s, s % FC
                ve.wait_ge(silu_done, T + 1)
                ve.wait_ge(u_ready, T + 1)
                reach(ve, lo_done, T - 3)
                ve.tensor_tensor(hid[:, c, :], act[:, c % 2, :], psU[c % 2][:, :], ALU.mult).then_inc(mul_done, 1)
                if not head or s >= 8:
                    add_piece(p, s)
                if not head or s > 0:
                    lo_part(p, s)

            def third_lo(p, r, third):
                par = (r + 1) % 2
                ve.wait_ge(whi_done, 6 * p + (3 * (r + 1) + third))
                at = SET_AT[par] + third * F
                split_lo(rbuf[:, at + WSET:at + WSET + F], raw[:, par, third * F:(third + 1) * F],
                         rbuf[:, at:at + F], wlo_done)

            def l1_weights(i):
                ve.wait_ge(tr_ready, i + 1)
                if i < 4:
                    dst = exT[:, 4 * i:4 * i + 4, :, :].rearrange("p e c n -> p c e n")
                    src = psX[i % 2][:, :].rearrange("p (c e n) -> p c e n", c=FC, e=4)
                elif i == 4:
                    dst = w2[:, 0, 0, :, 0:SHARED]
                    src = psX[0][:, 0:FC * SHARED].rearrange("p (c n) -> p c n", c=FC)
                else:
                    dst, src = fc1T[:, :], psX[1][:, :]
                ve.tensor_copy(dst, src).then_inc(tr_done, 1)

            def one_hot():
                ve.wait_ge(hot_ok, 1)
                ve.wait_ge(g_in, 16 * 8)
                ve.tensor_copy(row_f[:, :], row_id[:, :]).then_inc(hot_ok, 1)
                ve.tensor_copy(idxf[:, :, :], idxb[:, :, :]).then_inc(hot_ok, 1)
                ve.wait_ge(hot_ok, 3)
                ve.tensor_scalar(hot[:, :, :], idxf[:, :, :], row_f[:, 0:1], None, ALU.is_equal).then_inc(hot_ok, 1)

            def round_(p, r):
                for t in range(TILES):
                    s = TILES * r + t
                    slot(p, s, head=r == 0)
                    if r == 0:
                        if t == 0:
                            first_lo(2)
                        if t in X_TILE:
                            x_out(X_TILE.index(t) + 1)
                        if t - 1 in X_HI_TILE:
                            x_lo(X_HI_TILE.index(t - 1) + 1)
                        if t == 4:
                            weigh()
                        if t == 22:
                            one_hot()
                        if t - 1 in L1W_TILE:
                            l1_weights(L1W_TILE.index(t - 1))
                    if t % 8 == 2 and t > 8:
                        third_lo(p, r, t // 8 - 1)

            for i in range(2):
                x0_out(i)
            ve.wait_ge(first_in[0], 16)
            ve.tensor_copy(rbuf[:, SET_AT[0]:SET_AT[0] + F], raw[:, 0, 0:F]).then_inc(sg_hi, 1)
            first_lo(0)
            for i in range(2):
                x0_lo(i)
            first_lo(1)
            round_(0, 0)
            ve.wait_ge(bias_ready, 2)
            ve.tensor_copy(bias1[:, :], psX[0][:, 0:B]).then_inc(bias_ok, 1)
            ve.tensor_copy(bias2[:, :], psX[1][:, 0:B]).then_inc(bias_ok, 1)
            for a in range(2):
                ve.tensor_copy(g1b[:, a, :], g1s[:, a:a + 1].to_broadcast([P, P])).then_inc(g1b_ok, 1)
            ve.wait_ge(fc1hi_ok, 1)
            split_lo(fc1lo[:, :], fc1T[:, :], fc1hi[:, :], fc1lo_ok)
            with ve.Fori(0, NE // 2) as p:
                for r in (1, 2):
                    round_(p, r)

            def x1_lo(g):
                ve.wait_ge(x1hi, g)
                split_lo(xlo[:, bass.ds(g * GT, GT)], xT[:, bass.ds(g * GT, GT)], xhi[:, bass.ds(g * GT, GT)], x1lo)

            def residual(g, src, bias, done):
                for j in range(GB):
                    xb = xT[:, bass.ds(g * GT + j * P, P)]
                    ve.scalar_tensor_tensor(out=xb, in0=src[:, j * P:(j + 1) * P],
                                            scalar=bias[:, bass.ds(4 * g + j, 1)], in1=xb,
                                            op0=ALU.add, op1=ALU.add).then_inc(done, 1)

            def x3_lo(g, half):
                ve.wait_ge(xshi, g + 1)
                split_lo(xs_lo[:, half, :], xT[:, bass.ds(g * GT, GT)], xs_hi[:, half, :], xslo)

            def add_l1(g):
                ve.wait_ge(l1_ready, 4 * g + 4)
                residual(g, psY[g % 2], bias1, x2_done)

            def add_l2(g):
                ve.wait_ge(l2_ready, g + 1)
                residual(g, psX[g % 2], bias2, x3_done)

            def piece_lo(e, half, at_raw, count):
                ve.wait_ge(phi_done, count)
                at = EXP_AT + half * 2 * F
                split_lo(rbuf[:, e * EXP_STEP + (at + F):e * EXP_STEP + (at + 2 * F)], raw[:, half, at_raw:at_raw + F],
                         rbuf[:, e * EXP_STEP + at:e * EXP_STEP + (at + F)], plo_done)

            def l1_slot(g, half, e):
                if g >= 3:
                    add_l2(g - 3)
                if g + 2 < NG:
                    x1_lo(g + 2)
                piece_lo(e, half, 0, g + 1 + (2 if g > 1 else 0))
                if g == 1:
                    for w in range(2):
                        piece_lo(E3 - 1, w, F, 3 + w)
                if g == NG - 1:
                    x3_lo(0, 0)
                if g >= 1:
                    add_l1(g - 1)

            lo_part(0, TL0)
            x1_lo(1)
            for at in range(8):
                add_piece(0, TL0 + at)
            ve.wait_ge(bias_ok, 2)
            ve.wait_ge(y_added, TL0)
            for g in range(NG):
                l1_slot(g, g % 2, g // 2)

            def gate_columns(p):
                ve.wait_ge(s_out, 2 * p + 2)
                ve.tensor_copy(gS[:, :], ssb[:, bass.ds(p % 2 * 2, 2), :, 0:1].rearrange("p a j n -> p (a j n)")) \
                    .then_inc(gate_dve, 1)
                ve.wait_ge(gate_pe, 3 * p + 1)
                ve.tensor_copy(gE[:, :], psX[1][:, 0:2 * GB]).then_inc(gate_dve, 1)

            def gate_relu(p, ps=psX[1]):
                ve.wait_ge(gate_pe, 3 * p + 2)
                ve.tensor_scalar(ghid[:, :], ps[:, 8:8 + 2 * GB], 0.0, None, ALU.max).then_inc(gate_dve, 1)

            def gate_max(p, ps=psX[1]):
                ve.wait_ge(gate_pe, 3 * p + 3)
                ve.tensor_copy(glog[:, :, :], ps[:, 16:16 + 4 * GB].rearrange("p (a b) -> p a b", a=2)) \
                    .then_inc(gate_dve, 1)
                ve.wait_ge(gate_dve, GATE_STEPS * p + 4)
                ve.tensor_tensor(gmax[:, :], glog[:, 0, :], glog[:, 1, :], ALU.max).then_inc(gate_dve, 1)
                ve.wait_ge(gate_dve, GATE_STEPS * p + 5)
                ve.tensor_tensor(gdiff[:, :, :], glog[:, :, :], gmax[:, :].unsqueeze(1).to_broadcast([P, 2, 2 * GB]),
                                 ALU.subtract).then_inc(gate_dve, 1)

            def gate_weights(p):
                both = [P, 2, 2 * GB]
                ve.wait_ge(gate_act, p + 1)
                ve.tensor_scalar(gnum[:, :, :], gtanh[:, :, :], 1.0, None, ALU.add).then_inc(gate_dve, 1)
                ve.tensor_scalar(gden[:, :, :], gtanh[:, :, :], -1.0, 1.0, ALU.mult, ALU.add).then_inc(gate_dve, 1)
                ve.wait_ge(gate_dve, GATE_STEPS * p + 8)
                for a in range(2):
                    ve.tensor_tensor(gexp[:, a, :], gnum[:, a, :], gden[:, 1 - a, :], ALU.mult) \
                        .then_inc(*((gate_dve, 1) if a else (gate_half, 1)))
                ve.wait_ge(gate_half, p + 1)
                ve.wait_ge(gate_dve, GATE_STEPS * p + 9)
                ve.tensor_tensor(gsum[:, :], gexp[:, 0, :], gexp[:, 1, :], ALU.add).then_inc(gate_dve, 1)
                ve.wait_ge(gate_dve, GATE_STEPS * p + 10)
                ve.reciprocal(grec[:, :], gsum[:, :]).then_inc(gate_dve, 1)
                ve.wait_ge(gate_dve, GATE_STEPS * p + 11)
                ve.tensor_tensor(gw[:, :, :], gexp[:, :, :], grec[:, :].unsqueeze(1).to_broadcast(both), ALU.mult) \
                    .then_inc(gate_dve, 1)
                ve.wait_ge(gate_dve, GATE_STEPS * p + 12)

            def of_pair(buf, p, a, j):
                return buf[:, bass.ds(p % 2 * 2 + a, 1), j, :].rearrange("p a n -> p (a n)")

            def mix_shared(p, a):
                reach(ve, z_ready, 2 * p)
                for j in range(GB):
                    n = a * GB + j
                    ve.scalar_tensor_tensor(out=z[:, a, j, :], in0=of_pair(ssb, p, a, j), scalar=gw[:, 1, n:n + 1],
                                            in1=xT[:, bass.ds(p * (2 * GT) + n * P, P)],
                                            op0=ALU.mult, op1=ALU.add).then_inc(z_done, 1)

            def mix_expert(p, a):
                ve.wait_ge(z_ready, 2 * p + a + 1)
                reach(ve, out_sem[a], 16 * p)
                for j in range(GB):
                    n = a * GB + j
                    ve.scalar_tensor_tensor(out=osb[:, a, j, :], in0=of_pair(esb, p, a, j), scalar=gw[:, 0, n:n + 1],
                                            in1=psX[1][:, j * P:(j + 1) * P],
                                            op0=ALU.mult, op1=ALU.add).then_inc(o_done, 1)

            def mix(p, half, k):
                if (half, k) == (0, 6):
                    gate_columns(p)
                if (half, k) == (0, 7):
                    gate_relu(p)
                if (half, k) == (1, 0):
                    gate_max(p)
                if (half, k) == (1, 2):
                    gate_weights(p)
                    mix_shared(p, 0)
                if (half, k) == (1, 3):
                    mix_shared(p, 1)
                if (half, k) == (1, 5):
                    mix_expert(p, 0)
                if (half, k) == (1, 7):
                    mix_expert(p, 1)

            def rest_of_l1(k):
                if k == 1:
                    add_l2(NG - 2)
                if k == 3:
                    add_l1(NG - 1)
                if k == 5:
                    add_l2(NG - 1)

            def shared_lo(g, c):
                ve.wait_ge(shi, 4 * g + (c + 1))
                split_lo(shid(c, 1), hid[:, (2 * c + 1) % 4, :], shid(c, 0), slo)

            def l3_slot(g, half, p=None, first=False):
                for k in range(8):
                    K = 8 * g + k
                    ve.wait_ge(gelu3, K + 1)
                    ve.wait_ge(u3, K + 1)
                    if k % 2 == 0:
                        reach(ve, t_ready, 4 * g + (k // 2 - 1))
                    else:
                        reach(ve, slo, 4 * g + (k // 2 - 1))
                    ve.tensor_tensor(hid[:, k % 4, :], act[:, k % 2, :], psU[k % 2][:, :], ALU.mult).then_inc(mul3, 1)
                    if k % 2 == 0 and (not first or k >= 2):
                        shared_lo(*((g, k // 2 - 1) if k else (g - 1, FC - 1)))
                    if first:
                        rest_of_l1(k)
                    if p is not None:
                        mix(p, half, k)
                    if k == 5 and not (isinstance(g, int) and g == NG - 1):
                        x3_lo(g + 1, 1 - half)

            add_l2(NG - 3)
            l3_slot(0, 0, first=True)
            l3_slot(1, 1)
            with ve.Fori(1, NPAIR - 1) as p:
                for half in range(2):
                    l3_slot(2 * p + half, half, p - 1)
            for half in range(2):
                l3_slot(NG - 2 + half, half, NPAIR - 2)
            p = NPAIR - 1
            shared_lo(NG - 1, FC - 1)
            ve.wait_ge(s_out, NG)
            ve.tensor_copy(gS[:, :], ssb[:, LAST_RING:LAST_RING + 2, :, 0:1].rearrange("p a j n -> p (a j n)")) \
                .then_inc(gate_dve, 1)
            ve.wait_ge(last_turned, 1)
            ve.tensor_copy(gE[:, 0:GB], psX[1][:, :].rearrange("p (j n) -> p j n", j=GB)[:, :, 0])
            ve.wait_ge(gate_pe, 3 * p + 1)
            ve.tensor_copy(gE[:, GB:2 * GB], psX[0][:, :].rearrange("p (j n) -> p j n", j=GB)[:, :, 0]) \
                .then_inc(gate_dve, 1)
            gate_relu(p, psY[0])
            gate_max(p, psY[0])
            gate_weights(p)
            ve.wait_ge(last_turned, 5)
            ve.wait_ge(last_x3, 2)
            for a in range(2):
                ve.wait_ge(out_sem[a], 16 * p)
            for i in range(5):
                if i < 4:
                    for n in (2 * i, 2 * i + 1):
                        a, j = n // GB, n % GB
                        ve.scalar_tensor_tensor(out=part[:, a, j, :], in0=psU[a][:, j * P:(j + 1) * P],
                                                scalar=gw[:, 1, n:n + 1], in1=hid[:, 2 * a + 1, j * P:(j + 1) * P],
                                                op0=ALU.mult, op1=ALU.add).then_inc(z_done, 1)
                if i > 0:
                    a, j = (i - 1) // 2, (i - 1) % 2 * 2
                    ve.wait_ge(last_scaled, 2 * i)
                    ve.wait_ge(z_done, 8 * p + 2 * i)
                    ve.tensor_tensor(osb[:, a, j:j + 2, :], part[:, a, j:j + 2, :], last_e[:, a, j:j + 2, :], ALU.add) \
                        .then_inc(o_done, 1)

        @block.tensor
        def _(pe):
            def three(bank_, whi, wlo, mhi, mlo, start, stop):
                pe.matmul(bank_, whi, mhi, start=start, stop=False)
                pe.matmul(bank_, wlo, mhi, start=False, stop=False)
                return pe.matmul(bank_, whi, mlo, start=False, stop=stop)

            pe.wait_ge(ident_ok, 2)
            def x_turn(g):
                pe.wait_ge(x_in[g], 16)
                reach(pe, xt_done, g)
                for j in range(GB):
                    mm = pe.transpose(psX[g % 2][:, j * P:(j + 1) * P], xtok[:, g * GB + j, :], ident[:, :])
                mm.then_inc(xt_ready, 1)

            def down(p, s):
                T, c, half = 64 * p + s, s % FC, (s - 4) // FC % 2
                dpar = (s - 4) // TILES % 2
                pe.wait_ge(lo_done, T - 3)
                if c == 0:
                    reach(pe, y_added, T - 8)
                three(psY[half][:, :], wset(dpar, 0, 2, c), wset(dpar, 1, 2, c),
                      ring(half, c, 0), ring(half, c, 1), c == 0, c == FC - 1).then_inc(d_done, 1)

            def slot(p, s, head=False):
                T, c, wpar, col = 64 * p + s, s % FC, s // TILES % 2, s % TILES // FC * GT
                for q, bank_, free, done in ((0, psG, silu_done, g_ready), (1, psU, mul_done, u_ready)):
                    reach(pe, free, T - 1)
                    whi, wlo = wset(wpar, 0, q, c), wset(wpar, 1, q, c)
                    if head and s == 0:
                        pe.wait_ge(*((sg_hi, 1) if q == 0 else (whi_done, 1)))
                        pe.wait_ge(xhi_done, 2)
                        pe.matmul(bank_[0][:, :], whi, xhi[:, 0:GT], start=True, stop=False)
                        pe.wait_ge(wlo_done, q + 1)
                        pe.matmul(bank_[0][:, :], wlo, xhi[:, 0:GT], start=False, stop=False)
                        pe.wait_ge(xlo_done, 2)
                        pe.matmul(bank_[0][:, :], whi, xlo[:, 0:GT], start=False, stop=True).then_inc(done, 1)
                        continue
                    three(bank_[c % 2][:, :], whi, wlo,
                          xhi[:, col:col + GT], xlo[:, col:col + GT], True, True).then_inc(done, 1)
                if not head or s >= 4:
                    down(p, s)

            def l1_weights(i):
                reach(pe, tr_done, i - 1)
                for c in range(FC):
                    if i < 4:
                        mm = pe.transpose(psX[i % 2][:, c * P:(c + 1) * P], exraw[:, i, c * P:(c + 1) * P],
                                          ident[:, :])
                    elif i == 4:
                        mm = pe.transpose(psX[0][:, c * SHARED:(c + 1) * SHARED], fc2raw[:, c * P:(c + 1) * P],
                                          ident[0:SHARED, 0:SHARED])
                    else:
                        mm = pe.transpose(psX[1][:, c * P:(c + 1) * P], fc1raw[:, c, :], ident[:, :])
                mm.then_inc(tr_ready, 1)

            def keep_busy(n):
                for _ in range(n):
                    pe.transpose(psG[1][:, 0:P], ident[:, :], ident[:, :])

            keep_busy(WARM_UP[0])
            for i in range(2):
                pe.wait_ge(x0_in[i], 16)
                for j in range(2):
                    mm = pe.transpose((psX[0], psY[0])[i][:, j * P:(j + 1) * P], xtok[:, 2 * i + j, :], ident[:, :])
                mm.then_inc(xt_ready, 1)
            keep_busy(WARM_UP[1])
            for t in range(TILES):
                if t % FC == 0 and t > 0:
                    pe.wait_ge(xlo_done, t // FC + 2)
                if t == FC:
                    pe.wait_ge(wlo_done, 3)
                slot(0, t, head=True)
                if t in X_TILE:
                    x_turn(X_TILE.index(t) + 1)
                if t == L1W_TILE[0]:
                    pe.wait_ge(l1w_in, 48)
                    pe.wait_ge(xt_done, NG + 1)
                if t in L1W_TILE:
                    l1_weights(L1W_TILE.index(t))
            pe.wait_ge(hot_ok, 4)
            pe.wait_ge(tr_done, 6)
            pe.matmul(psX[0][:, 0:B], table1[:, :], hot[0:E1, 0, :], start=True, stop=True).then_inc(bias_ready, 1)
            pe.matmul(psX[1][:, 0:B], table2[:, :], hot[:, 1, :], start=True, stop=True).then_inc(bias_ready, 1)

            with pe.Fori(0, NE // 2) as p:
                for r in (1, 2):
                    pe.wait_ge(wlo_done, 6 * p + 3 * (r + 1))
                    for t in range(TILES):
                        slot(p, TILES * r + t)
            def l1_down(g, half, c):
                if c == 0:
                    pe.wait_ge(gelu_done, 4 * g + 4)
                    if isinstance(g, int) and g == 0:
                        pe.wait_ge(y_added, TL0)
                    else:
                        reach(pe, x2_done, 4 * g - 4)
                pe.wait_ge(w2_ready, 4 * g + (c + 1))
                for i in range(FC):
                    mm = pe.matmul(psY[half][:, c * P:(c + 1) * P], w2[:, half, c, i, :],
                                   h1[:, half, i, c * P:(c + 1) * P], start=i == 0, stop=i == FC - 1)
                mm.then_inc(l1_ready, 1)

            def l2(g, half, p):
                pe.wait_ge(x2_done, 4 * g + 4)
                pe.wait_ge(cat_in[half], 64 * p)
                for j in range(GB):
                    mm = pe.matmul(psX[half][:, j * P:(j + 1) * P], wcat[:, half, j, :],
                                   xT[:, bass.ds(g * GT + j * P, P)], start=True, stop=True)
                mm.then_inc(l2_ready, 1)

            def fc1(c):
                return fc1hi[:, c * P:(c + 1) * P], fc1lo[:, c * P:(c + 1) * P]

            def last_downs():
                pe.wait_ge(fc1lo_ok, 1)
                pe.wait_ge(x1_first, 2)
                for kind, c in (("fc1", 0), ("fc1", 1), ("down", 0), ("down", 1), ("down", 2), ("down", 3),
                                ("fc1", 2), ("fc1", 3)):
                    if kind == "down":
                        down(0, TL0 + c)
                        continue
                    pe.wait_ge(*((silu_done, TL0 - 1 + c) if c < 2 else (gelu_done, c - 1)))
                    three(psG[c % 2][:, :], *fc1(c), xhi[:, 0:GT], xlo[:, 0:GT], True, True).then_inc(fc_ready, 1)

            def l1_slot(g, half, p):
                for c in range(FC):
                    if c == 0:
                        pe.wait_ge(x1lo, g)
                    reach(pe, gelu_done, 4 * g + (c - 1))
                    three(psG[c % 2][:, :], *fc1(c),
                          xhi[:, bass.ds(g * GT, GT)], xlo[:, bass.ds(g * GT, GT)], True, True) \
                        .then_inc(fc_ready, 1)
                    l1_down(g - 1, 1 - half, c)
                if not isinstance(g, int):
                    l2(g - 2, half, p)

            last_downs()
            pe.wait_ge(bias_ok, 2)
            pe.wait_ge(fc2_ok, 2 * GB - 1)
            l1_slot(1, 1, 0)
            with pe.Fori(1, NPAIR) as p:
                for half in range(2):
                    l1_slot(2 * p + half, half, p)

            def expert_of(g, j):
                return pe.value_load(idxs[0:1, 2, bass.ds(4 * g + j, 1)], min_val=0, max_val=E3 - 1)

            def expert_in(g, half, j):
                n = expert_of(g, j)
                mhi, mlo = xs_hi[:, half, j * P:(j + 1) * P], xs_lo[:, half, j * P:(j + 1) * P]
                for bank_, w, free, done in ((psG, 0, gelu3, g3), (psU, 1, mul3, u3)):
                    reach(pe, free, 8 * g + (2 * j - 1))
                    whi = rbuf[:, bass.ds(n * EXP_STEP + (EXP_AT + w * 2 * F), F)]
                    wlo = rbuf[:, bass.ds(n * EXP_STEP + (EXP_AT + w * 2 * F + F), F)]
                    three(bank_[0][:, :], mhi, mlo, whi, wlo, True, True).then_inc(done, 1)

            def shared_in(g, half, c):
                for bank_, q, free, done in ((psG, 0, gelu3, g3), (psU, 1, mul3, u3)):
                    reach(pe, free, 8 * g + 2 * c)
                    three(bank_[1][:, :], wset(1, 0, q, c), wset(1, 1, q, c), xs_hi[:, half, :], xs_lo[:, half, :],
                          True, True).then_inc(done, 1)

            def shared_down(g, c):
                pe.wait_ge(slo, 4 * g + (c + 1))
                if c == 0:
                    reach(pe, s_out, g)
                mm = three(psY[0][:, :], wset(1, 0, 2, c), wset(1, 1, 2, c), shid(c, 0), shid(c, 1),
                           c == 0, c == FC - 1)
                mm.then_inc(d_done, 1)

            def turn(g, j):
                pe.wait_ge(mul3, 8 * g + (2 * j + 1))
                reach(pe, t_out, 4 * g + j)
                for c in range(FC):
                    mm = pe.transpose(psX[0][:, c * P:(c + 1) * P], hid[:, 2 * j % 4, c * P:(c + 1) * P],
                                      ident[:, :])
                mm.then_inc(t_ready, 1)

            def expert_down(g, j):
                n = expert_of(g, j)
                pe.wait_ge(t_out, 4 * g + (j + 1))
                if j == 0:
                    reach(pe, e_out, g)
                for c in range(FC):
                    mm = pe.matmul(psY[1][:, j * P:(j + 1) * P], hT[:, j % 2, c * P:(c + 1) * P],
                                   woe[:, bass.ds(n, 1), c, :].rearrange("p a n -> p (a n)"),
                                   start=c == 0, stop=c == FC - 1)
                mm.then_inc(e_done, 1)

            def gate_shared(p, ps=psX[1], steps=2):
                pe.wait_ge(gate_dve, GATE_STEPS * p + steps)
                pe.matmul(ps[:, 8:8 + 2 * GB], g0s[:, 1, :], gS[:, :], start=True, stop=False)

            def gate_expert(p, ps=psX[1]):
                pe.wait_ge(gate_dve, GATE_STEPS * p + 2)
                pe.matmul(ps[:, 8:8 + 2 * GB], g0s[:, 0, :], gE[:, :], start=False, stop=True).then_inc(gate_pe, 1)

            def gate_logits(p, ps=psX[1]):
                pe.wait_ge(gate_dve, GATE_STEPS * p + 3)
                for a in range(2):
                    mm = pe.matmul(ps[:, 16 + a * 2 * GB:16 + (a + 1) * 2 * GB], g1b[:, a, :], ghid[:, :],
                                   start=True, stop=True)
                mm.then_inc(gate_pe, 1)

            def mix(p, half, k):
                if (half, k) == (0, 6):
                    pe.wait_ge(e0_in, 16 * p + 16)
                    reach(pe, o_done, 8 * p)
                    pe.matmul(psX[1][:, 0:2 * GB], e0r[:, :], ident[0:2 * GB, 0:2 * GB], start=True,
                              stop=True).then_inc(gate_pe, 1)
                if (half, k) == (0, 7):
                    gate_shared(p)
                    gate_expert(p)
                if (half, k) == (1, 0):
                    gate_logits(p)
                for a in range(2):
                    if (half, k) == (1, 4 + 2 * a):
                        pe.wait_ge(z_done, 8 * p + (4 * a + 4))
                        reach(pe, o_done, 8 * p + 4 * a)
                        for j in range(GB):
                            mm = pe.transpose(psX[1][:, j * P:(j + 1) * P], z[:, a, j, :], ident[:, :])
                        mm.then_inc(z_ready, 1)

            def l3_slot(g, half, p=None, first=False):
                for k in range(8):
                    if k == 0:
                        pe.wait_ge(xslo, g + 1)
                    (shared_in if k % 2 else expert_in)(g, half, k // 2)
                    if first:
                        rest_of_l1(k)
                    if k % 2 == 1 and (not first or k >= 3):
                        shared_down(*((g, k // 2 - 1) if k >= 3 else (g - 1, FC - 1)))
                    if k % 2 == 0:
                        if not first or k >= 4:
                            expert_down(*((g, k // 2 - 2) if k >= 4 else (g - 1, k // 2 + 2)))
                        if not first or k >= 2:
                            turn(*((g, k // 2 - 1) if k >= 2 else (g - 1, GB - 1)))
                    if p is not None:
                        mix(p, half, k)

            def rest_of_l1(k):
                if k < GB:
                    l1_down(NG - 1, 1, k)
                if k == 1:
                    l2(NG - 2, 0, NPAIR)
                    pe.wait_ge(x2_done, 4 * (NG - 1))
                if k == 2:
                    pe.wait_ge(x3_done, 4 * (NG - 1))
                if k == 4:
                    l2(NG - 1, 1, NPAIR)

            pe.wait_ge(plo_done, 2 * E3)
            pe.wait_ge(wo_in, 16 * E3)
            pe.wait_ge(gelu_done, TILES)
            pe.wait_ge(g1b_ok, 2)
            l3_slot(0, 0, first=True)
            l3_slot(1, 1)
            with pe.Fori(1, NPAIR - 1) as p:
                for half in range(2):
                    l3_slot(2 * p + half, half, p - 1)
            for half in range(2):
                l3_slot(NG - 2 + half, half, NPAIR - 2)

            def turn_last(bank_, src):
                for j in range(GB):
                    mm = pe.transpose(bank_[:, j * P:(j + 1) * P], src(j), ident[:, :])
                return mm

            p = NPAIR - 1
            turn(NG - 1, GB - 1)
            expert_down(NG - 1, 2)
            pe.wait_ge(o_done, 8 * p)
            pe.wait_ge(e_out, NG - 1)
            turn_last(psX[1], lambda j: esb[:, LAST_RING, j, :]).then_inc(last_turned, 1)
            pe.wait_ge(mul3, 8 * NG)
            pe.wait_ge(s_out, NG - 1)
            turn_last(psU[0], lambda j: ssb[:, LAST_RING, j, :]).then_inc(last_turned, 1)
            expert_down(NG - 1, GB - 1)
            shared_down(NG - 1, FC - 1)
            pe.wait_ge(e_out, NG)
            turn_last(psX[0], lambda j: esb[:, LAST_RING + 1, j, :]).then_inc(gate_pe, 1)
            gate_shared(p, psY[0], 1)
            gate_expert(p, psY[0])
            pe.wait_ge(gelu3, 8 * NG)
            turn_last(psG[0], lambda j: xT[:, (8 * p + j) * P:(8 * p + j + 1) * P]).then_inc(last_turned, 1)
            gate_logits(p, psY[0])
            turn_last(psG[1], lambda j: xT[:, (8 * p + GB + j) * P:(8 * p + GB + j + 1) * P]).then_inc(last_turned, 1)
            turn_last(psU[1], lambda j: ssb[:, LAST_RING + 1, j, :]).then_inc(last_turned, 1)


_INS = ['x', 'fside_Bx8_0', 'condB_sharedgateprob', 'itok_B_0_15', 'itok_B_0_63', 'itok_B_0_2',
        'L0_cond_Wg', 'L0_cond_Wu', 'L0_cond_Wd', 'L0_cond_Sg', 'L0_cond_Su', 'L0_cond_Sd',
        'L1_cond_fc1_w', 'L1_cond_fc1_b', 'L1_cond_fc2_w', 'L1_cond_fc2_b', 'L1_cond_experts_w', 'L1_cond_experts_b',
        'L2_cond_W', 'L2_cond_b', 'L3_cond_Wi0', 'L3_cond_Wi1', 'L3_cond_Wo',
        'L3_cond_sWi0', 'L3_cond_sWi1', 'L3_cond_sWo', 'L3_cond_g0', 'L3_cond_g1']


def kernel(**inputs):
    import numpy as np
    import concourse.bacc as bacc
    from concourse import mybir as mb
    from concourse.bass_utils import run_bass_kernel_spmd

    nc = bacc.Bacc("TRN2", target_bir_lowering=False, num_devices=1)
    arrays, args = {}, []
    for name in _INS:
        a = np.ascontiguousarray(inputs[name])
        arrays[f"in_{name}"] = a
        args.append(nc.dram_tensor(f"in_{name}", a.shape, mb.dt.from_np(a.dtype), kind="ExternalInput").ap())
    result = nc.dram_tensor("out_x", (B, P, P), mb.dt.float32, kind="ExternalOutput").ap()
    build_kernel(nc, *args, result)
    r = run_bass_kernel_spmd(nc, [arrays], core_ids=[0])
    return r.results[0]["out_x"]
```
